# Optimizing a Trainium2 kernel written in Bass

```python
import numpy as np
import jax
import jax.numpy as jnp

def _softmax(x, axis=-1):
    return jax.nn.softmax(x, axis=axis)

def _gelu(x):
    return jax.nn.gelu(x, approximate=True)

def _silu(x):
    return jax.nn.silu(x)

def _sigmoid(x):
    return jax.nn.sigmoid(x)

def _layernorm(x, axis=-1, eps=1e-05):
    m = jnp.mean(x, axis=axis, keepdims=True)
    v = jnp.var(x, axis=axis, keepdims=True)
    return (x - m) / jnp.sqrt(v + eps)

def _scatter_add(tgt, idx, src, axis=0):
    return tgt.at[idx].add(src)

def _segment_sum(src, seg, n):
    return jax.ops.segment_sum(src, seg, n)
kernel_name = 'mk_flamingo_gated_d1_seqx_r8_667950'

def setup_inputs(seed: int=0):
    np.random.seed(seed)
    _w = jnp.asarray

    def _rec_inputs():
        import jax
        import jax.numpy as jnp
        _rk = jax.random.key(seed)
        x = -7.109e-05 + 0.9999 * jax.random.normal(jax.random.fold_in(_rk, 1), (4, 256, 256), jnp.float32)
        _lenS = 256 - jax.random.randint(jax.random.fold_in(_rk, 7), (4,), 0, max(1, 256 // 4) + 1, jnp.int32)
        _lenS2 = 256 - jax.random.randint(jax.random.fold_in(_rk, 8), (4,), 0, max(1, 256 // 4) + 1, jnp.int32)
        _ctx_512P = jax.random.normal(jax.random.fold_in(_rk, 11), (4, 16, 64), jnp.float32)
        _ctx_512c = jax.random.dirichlet(jax.random.fold_in(_rk, 511), 0.3 * jnp.ones((16,), jnp.float32), (4, 256))
        _ctx_512t = jnp.einsum('bsk,bkd->bsd', _ctx_512c, _ctx_512P)
        _ctx_512t = _ctx_512t * jax.lax.rsqrt(jnp.mean(jnp.square(_ctx_512t)) + 1e-12) * 0.953939
        ctx_512 = 2.81802e-05 + 1.00001 * (_ctx_512t + 0.3 * jax.random.normal(jax.random.fold_in(_rk, 611), (4, 256, 64), jnp.float32))
        _g = jax.random.normal(jax.random.fold_in(_rk, 9001), (2, 1), jnp.float32)
        _g = jnp.sign(_g) * jnp.maximum(jnp.abs(_g), 1.0) + (_g == 0) * 1.0
        g_xattn = _g[0]
        g_ffn = _g[1]
        return (x, ctx_512, g_xattn, g_ffn)
    x, ctx_512, g_xattn, g_ffn = _rec_inputs()

    def _L0_xattn_setup():
        import jax, jax.numpy as jnp
        import numpy as np
        EPS = 1e-06
        IMAGE_DIMS = 256
        key = jax.random.key(seed)
        k1, k2, k3 = jax.random.split(key, 3)
        B, I, J, D = (16, 256, 256, 64)
        p = jax.random.normal(k1, (B, I, J), dtype=jnp.float32)
        k_v = jax.random.normal(k2, (B, J, D), dtype=jnp.float32)
        W_k = jax.random.normal(k3, (D, D), dtype=jnp.float32) * (1.0 / np.sqrt(D))
        b_k = jnp.zeros((D,), dtype=jnp.float32)
        ln_gamma = jnp.ones((J,), dtype=jnp.float32)
        ln_beta = jnp.zeros((J,), dtype=jnp.float32)
        return {'p': p, 'k_v': k_v, 'W_k': W_k, 'b_k': b_k, 'ln_gamma': ln_gamma, 'ln_beta': ln_beta}
    _L0_xattn_all = _L0_xattn_setup()
    _L0_xattn_in = {k: v for k, v in _L0_xattn_all.items() if k in ('W_k', 'b_k', 'ln_gamma', 'ln_beta')}
    del _L0_xattn_all

    def _L0_ffn_setup():
        import jax, jax.numpy as jnp
        import numpy as np
        B, S, D, F, E, K = (2, 256, 256, 1024, 8, 2)
        key = jax.random.key(seed)
        k0, k1, k2, k3 = jax.random.split(key, 4)
        scale = lambda k, shape, fan_in: jax.random.normal(k, shape, jnp.float32) * fan_in ** (-0.5)
        return {'inputs': jax.random.normal(k0, (B, S, D), jnp.float32), 'gate_w': scale(k1, (D, E), D), 'gate_b': jnp.zeros((E,), jnp.float32), 'w1': scale(k2, (E, D, F), D), 'b1': jnp.zeros((E, F), jnp.float32), 'w2': scale(k3, (E, F, D), F), 'b2': jnp.zeros((E, D), jnp.float32)}
    _L0_ffn_all = _L0_ffn_setup()
    _L0_ffn_in = {k: v for k, v in _L0_ffn_all.items() if k in ('gate_w', 'gate_b', 'w1', 'b1', 'w2', 'b2')}
    del _L0_ffn_all
    return {'x': x, 'ctx_512': ctx_512, 'g_xattn': g_xattn, 'g_ffn': g_ffn, 'L0_xattn_W_k': _L0_xattn_in['W_k'], 'L0_xattn_b_k': _L0_xattn_in['b_k'], 'L0_xattn_ln_gamma': _L0_xattn_in['ln_gamma'], 'L0_xattn_ln_beta': _L0_xattn_in['ln_beta'], 'L0_ffn_gate_w': _L0_ffn_in['gate_w'], 'L0_ffn_gate_b': _L0_ffn_in['gate_b'], 'L0_ffn_w1': _L0_ffn_in['w1'], 'L0_ffn_b1': _L0_ffn_in['b1'], 'L0_ffn_w2': _L0_ffn_in['w2'], 'L0_ffn_b2': _L0_ffn_in['b2']}

def reference(x, ctx_512, g_xattn, g_ffn, L0_xattn_W_k, L0_xattn_b_k, L0_xattn_ln_gamma, L0_xattn_ln_beta, L0_ffn_gate_w, L0_ffn_gate_b, L0_ffn_w1, L0_ffn_b1, L0_ffn_w2, L0_ffn_b2):
    import jax
    import jax.numpy as jnp

    def _L0_xattn_ref(p, k_v, W_k, b_k, ln_gamma, ln_beta):
        import jax, jax.numpy as jnp
        import numpy as np
        EPS = 1e-06
        IMAGE_DIMS = 256
        kv = k_v @ W_k.T + b_k
        out = jnp.einsum('bij,bjd->bid', p, kv)
        scale = IMAGE_DIMS ** (-0.5)
        sim = jnp.einsum('bid,bjd->bij', out, kv) * scale
        mu = jnp.mean(sim, axis=-1, keepdims=True)
        var = jnp.var(sim, axis=-1, keepdims=True)
        sim = (sim - mu) * jax.lax.rsqrt(var + EPS) * ln_gamma + ln_beta
        attn = jax.nn.softmax(sim, axis=-1)
        return attn

    def _L0_ffn_ref(inputs, gate_w, gate_b, w1, b1, w2, b2):
        import jax, jax.numpy as jnp
        import numpy as np
        B, S, D, F, E, K = (2, 256, 256, 1024, 8, 2)
        x = inputs.reshape(-1, inputs.shape[-1])
        n = x.shape[0]
        gate_probs = jax.nn.softmax(x @ gate_w + gate_b, axis=-1)
        weights, selected = jax.lax.top_k(gate_probs, K)
        weights = weights / jnp.sum(weights, axis=-1, keepdims=True)
        comb = jnp.zeros((n, E), x.dtype).at[jnp.arange(n)[:, None], selected].set(weights)
        h = jax.nn.gelu(jnp.einsum('nd,edf->enf', x, w1) + b1[:, None, :])
        expert_out = jnp.einsum('enf,efd->end', h, w2) + b2[:, None, :]
        out = jnp.einsum('ne,end->nd', comb, expert_out)
        return out.reshape(inputs.shape[:-1] + (out.shape[-1],))
    x = x + jnp.tanh(g_xattn[0]) * _L0_xattn_ref(_layernorm(x, axis=-1), ctx_512, L0_xattn_W_k, L0_xattn_b_k, L0_xattn_ln_gamma, L0_xattn_ln_beta)
    x = x + jnp.tanh(g_ffn[0]) * _L0_ffn_ref(_layernorm(x, axis=-1), L0_ffn_gate_w, L0_ffn_gate_b, L0_ffn_w1, L0_ffn_b1, L0_ffn_w2, L0_ffn_b2)
    return x

_drawn_inputs = setup_inputs


def setup_inputs(seed=0):
    import zlib

    import numpy as np

    out = dict(_drawn_inputs(seed))
    spreads = {'L0_xattn_b_k': (0.0, 0.8),
     'L0_xattn_ln_gamma': (1.0, 0.6),
     'L0_xattn_ln_beta': (0.0, 0.8),
     'L0_ffn_gate_b': (0.0, 0.1),
     'L0_ffn_b1': (0.0, 0.1),
     'L0_ffn_b2': (0.0, 0.1)}
    factors = {'ctx_512': 3.077, 'L0_xattn_W_k': 4.903}
    for name, (base, spread) in spreads.items():
        noise = np.random.default_rng([zlib.crc32(name.encode()), seed]).standard_normal(out[name].shape)
        drawn = base * np.exp(spread * noise) if base else spread * noise
        out[name] = jnp.asarray(drawn.astype(out[name].dtype))
    for name, factor in factors.items():
        out[name] = (out[name] * factor).astype(out[name].dtype)
    return out
```

```python
from contextlib import ExitStack

import numpy as np

import concourse.bass as bass
from concourse import mybir

ALU = mybir.AluOpType
ACT = mybir.ActivationFunctionType
F32 = mybir.dt.float32
F16 = mybir.dt.float16
I32 = mybir.dt.int32
U32 = mybir.dt.uint32
P = 128

X_SCALE = 2.0 ** 10
W_SCALE = 2.0 ** 10
H_SCALE = 2.0 ** 6
LN_EPS = 1e-5
SIM_EPS = 1e-6


def gated_block(nc, x, ctx_kv, g_xattn, g_ffn, w_k, b_k, ln_gamma, ln_beta,
                gate_w, gate_b, w1, b1, w2, b2, out):
    B, S, D = x.shape
    C = ctx_kv.shape[2]
    E, _, F = w1.shape
    N = B * S
    TT = N // P
    HB = S // P
    DC = D // P
    FC = F // P
    KTOP = 2
    JT = N // P
    SLOTS = E * N
    MAXT = (KTOP * N + E * (P - 1)) // P
    PAD = P
    STG = 3
    CH = DC * F
    assert DC * F == FC * D and S == D and HB == 2 and DC == 2 and FC == 8 and E == 8

    xn_rows = nc.dram_tensor("xn_rows", (N + PAD, D), F32).ap()
    table = nc.dram_tensor("table", (SLOTS, 2), I32).ap()

    es = ExitStack()
    with es:
        def sb(name, shape, dt):
            return es.enter_context(nc.sbuf_tensor(name, shape, dt))

        def sem(name):
            return es.enter_context(nc.semaphore(name))

        bank = [es.enter_context(nc.psum_tensor(f"bank{i}", [P, 512], F32)) for i in range(8)]

        whi = sb("whi", [P, E, 2, CH], F16)
        wlo = sb("wlo", [P, E, 2, CH], F16)
        stage = sb("stage", [P, STG, CH], F32)
        xs = sb("xs", [P, TT, D], F32)
        xn = sb("xn", [P, TT, D], F32)
        ctx_sb = sb("ctx_sb", [P, TT, C], F32)
        ctxT = sb("ctxT", [C + 1, N], F32)
        wk_sb = sb("wk_sb", [C, C], F32)
        wkT = sb("wkT", [C + 1, C], F32)
        kvT = sb("kvT", [C, N], F32)
        kv = sb("kv", [P, TT, C], F32)
        pT = sb("pT", [P, DC, S], F32)
        outT = sb("outT", [C, S], F32)
        sim = sb("sim", [P, 2, HB, S], F32)
        negbeta = sb("negbeta", [P, S], F32)
        gamma = sb("gamma", [P, S], F32)
        x2T = sb("x2T", [P, DC, S], F32)
        gw = sb("gw", [P, DC, E], F32)
        gb = sb("gb", [P, E], F32)
        b2_sb = sb("b2_sb", [E, D], F32)
        b1_rows = sb("b1_rows", [E * FC, P], F32)
        b1_sb = sb("b1_sb", [P, E * FC], F32)
        gates = sb("gates", [P, 2], F32)
        gslot = sb("gslot", [P, 1], F32)
        ident = sb("ident", [P, P], F32)
        before = sb("before", [P, P], F32)
        ones = sb("ones", [P, P], F32)
        zeros = sb("zeros", [P, D], F32)
        halfneg = sb("halfneg", [P, 8], F32)
        st = sb("st", [P, 3, TT, 6], F32)
        mv = sb("mv", [P, 3, TT, 2], F32)
        veps = sb("veps", [P, 3, TT], F32)
        rstd = sb("rstd", [P, 3, TT], F32)
        nrs = sb("nrs", [P, TT], F32)
        mrs = sb("mrs", [P, TT], F32)
        negmax = sb("negmax", [P, TT], F32)
        esum = sb("esum", [P, TT], F32)
        rsum = sb("rsum", [P, TT], F32)
        coef = sb("coef", [P, TT], F32)
        lg = sb("lg", [P, TT, E], F32)
        mx = sb("mx", [P, TT, 8], F32)
        ix = sb("ix", [P, TT, 8], U32)
        ixf = sb("ixf", [P, TT, KTOP], F32)
        iota_e = sb("iota_e", [P, E], F32)
        dif = sb("dif", [P, TT], F32)
        e2 = sb("e2", [P, TT], F32)
        den = sb("den", [P, TT], F32)
        wk2 = sb("wk2", [P, TT, KTOP], F32)
        mask = sb("mask", [P, TT, KTOP, E], F32)
        mcount = sb("mcount", [P, TT, E], F32)
        msum = sb("msum", [P, TT + 1, E], F32)
        wmask = sb("wmask", [P, TT, KTOP, E], F32)
        comb = sb("comb", [P, TT, E], F32)
        combT = sb("combT", [E, HB * P], F32)
        rmask = sb("rmask", [P, TT, KTOP, E], F32)
        rankf = sb("rankf", [P, TT, KTOP], F32)
        ranki = sb("ranki", [P, TT, KTOP], I32)
        rlow = sb("rlow", [P, TT, KTOP], I32)
        rrow = sb("rrow", [P, TT, KTOP], I32)
        slot = sb("slot", [P, TT, KTOP], I32)
        entry = sb("entry", [P, TT, KTOP, 2], I32)
        meta = sb("meta", [P, E * JT, 2], I32)
        cnti = sb("cnti", [1, E], I32)
        cntr = sb("cntr", [1, E], I32)
        ntile = sb("ntile", [1, E], I32)
        ntf = sb("ntf", [1, E], F32)
        zer8 = sb("zer8", [1, E], F32)
        cend = sb("cend", [1, E], F32)
        cendi = sb("cendi", [1, E], I32)
        giota = sb("giota", [1, MAXT + 2], F32)
        past = sb("past", [1, MAXT + 2, E], F32)
        pastn = sb("pastn", [1, MAXT + 2, E], F32)
        eg = sb("eg", [1, MAXT + 2], F32)
        sg = sb("sg", [1, MAXT + 2], F32)
        col1 = sb("col1", [1, MAXT + 2], F32)
        col2 = sb("col2", [1, MAXT + 2], F32)
        coli = sb("coli", [1, MAXT + 2], I32)
        egi = sb("egi", [1, MAXT + 2], I32)
        gidx = sb("gidx", [P, 1], I32)
        sidx = sb("sidx", [P, 1], I32)
        xhi = sb("xhi", [P, DC, P], F16)
        xlo = sb("xlo", [P, DC, P], F16)
        hact = xn[:, 0:4, :].rearrange("p a b -> p (a b)").rearrange("p (f t) -> p f t", f=FC)
        hhi = xn[:, 4:6, :].bitcast(F16).rearrange("p a b -> p (a b)").rearrange("p (f t) -> p f t", f=FC)
        hlo = xn[:, 6:8, :].bitcast(F16).rearrange("p a b -> p (a b)").rearrange("p (f t) -> p f t", f=FC)
        xg = ctx_sb[:, 0:4, :].rearrange("p a b -> p (a b)")
        ysb = ctx_sb[:, 4:8, :].rearrange("p a b -> p (a b)")

        x_in = [sem(f"x_in{b}") for b in range(B)]
        ctx_in = sem("ctx_in")
        small_in = sem("small_in")
        pads_out = sem("pads_out")
        w_in = [sem(f"w_in{i}") for i in range(STG)]
        consts = sem("consts")
        wk_t = sem("wk_t")
        wkT_ok = sem("wkT_ok")
        b1_t = sem("b1_t")
        b1_ok = sem("b1_ok")
        ctx_t = sem("ctx_t")
        ctxT_ok = sem("ctxT_ok")
        kv_mm = sem("kv_mm")
        kv_ok = sem("kv_ok")
        tanh_ok = sem("tanh_ok")
        dve_step = sem("dve_step")
        pool_step = sem("pool_step")
        mv1_ok = sem("mv1_ok")
        rstd1_ok = sem("rstd1_ok")
        xn1_ok = sem("xn1_ok")
        p_t = sem("p_t")
        pT_ok = sem("pT_ok")
        out_mm = sem("out_mm")
        outT_ok = sem("outT_ok")
        sim_mm = sem("sim_mm")
        mv2_ok = sem("mv2_ok")
        rstd2_ok = sem("rstd2_ok")
        simn_ok = sem("simn_ok")
        aff_ok = sem("aff_ok")
        exp_ok = sem("exp_ok")
        mv3_ok = sem("mv3_ok")
        rstd3_ok = sem("rstd3_ok")
        xn2_ok = sem("xn2_ok")
        rows_out = sem("rows_out")
        x2_t = sem("x2_t")
        x2T_ok = sem("x2T_ok")
        lg_mm = sem("lg_mm")
        dif_ok = sem("dif_ok")
        e2_ok = sem("e2_ok")
        mask_ok = sem("mask_ok")
        rank_mm = sem("rank_mm")
        slot_ok = sem("slot_ok")
        entry_out = sem("entry_out")
        comb_ok = sem("comb_ok")
        comb_t = sem("comb_t")
        combT_ok = sem("combT_ok")
        b2_mm = sem("b2_mm")
        res_ok = sem("res_ok")
        res_out = sem("res_out")
        hi_ok = sem("hi_ok")
        lo_ok = sem("lo_ok")
        cnt_mm = sem("cnt_mm")
        plan_ok = sem("plan_ok")
        meta_in = sem("meta_in")
        gidx_ok = sem("gidx_ok")
        xg_in = sem("xg_in")
        xg_t = sem("xg_t")
        xhi_ok = sem("xhi_ok")
        xlo_ok = sem("xlo_ok")
        h_mm = sem("h_mm")
        act_ok = sem("act_ok")
        hhi_ok = sem("hhi_ok")
        hsplit_ok = sem("hsplit_ok")
        y_mm = sem("y_mm")
        y_ok = sem("y_ok")
        sidx_ok = sem("sidx_ok")
        added = sem("added")
        ysb_free = sem("ysb_free")

        NSMALL = 10
        STEPS = B + 3
        NW = 2 * E
        EARLY = 4

        def w_dram(n):
            e, which = divmod(n, 2)
            src = w2 if which else w1
            return src[e].rearrange("(c p) n -> p c n", p=P)

        def w_stage(n, lo=0, hi=CH):
            return stage[:, n % STG, lo:hi]

        block = es.enter_context(nc.Block())

        @block.sync
        def _(sp):
            for b in range(B):
                sp.dma_start(xs[:, HB * b:HB * b + HB, :],
                             x[b].rearrange("(h p) d -> p h d", p=P)).then_inc(x_in[b], 16)
            for n in range(NW):
                if n == EARLY + STG:
                    sp.wait_ge(entry_out, 16 * TT * KTOP)
                    sp.dma_start(meta[:, :, :], table.rearrange("(p c) k -> p c k", p=P)).then_inc(meta_in, 16)
                if n >= STG:
                    sp.wait_ge(hi_ok, 4 * (n - STG + 1))
                    sp.wait_ge(lo_ok, 4 * (n - STG + 1))
                c = DC if n % 2 == 0 else FC
                sp.dma_start(w_stage(n).rearrange("p (c n) -> p c n", c=c), w_dram(n)).then_inc(w_in[n % STG], 16)
        @block.scalar
        def _(act):
            act.dma_start(ctx_sb[:, :, :], ctx_kv.rearrange("b (h p) c -> p (b h) c", p=P)).then_inc(ctx_in, 16)
            act.dma_start(wk_sb[:, :], w_k).then_inc(small_in, 16)
            act.dma_start(wkT[C:C + 1, :], b_k.unsqueeze(0)).then_inc(small_in, 16)
            act.dma_start(gates[:, 0:1], g_xattn.partition_broadcast(P)).then_inc(small_in, 16)
            act.dma_start(gates[:, 1:2], g_ffn.partition_broadcast(P)).then_inc(small_in, 16)
            act.dma_start(gamma[:, :], ln_gamma.partition_broadcast(P)).then_inc(small_in, 16)
            act.dma_start(negbeta[:, :], ln_beta.partition_broadcast(P)).then_inc(small_in, 16)
            act.dma_start(gw[:, :, :], gate_w.rearrange("(c p) e -> p c e", p=P)).then_inc(small_in, 16)
            act.dma_start(gb[:, :], gate_b.partition_broadcast(P)).then_inc(small_in, 16)
            act.dma_start(b2_sb[:, :], b2).then_inc(small_in, 16)
            act.dma_start(b1_rows[:, :], b1.rearrange("e (c p) -> (e c) p", p=P)).then_inc(small_in, 16)

            act.wait_ge(small_in, 16 * NSMALL)
            nc.scalar.activation(gates[:, :], gates[:, :], ACT.Tanh).then_inc(tanh_ok, 1)
            act.wait_ge(wk_t, 1)
            nc.scalar.copy(wkT[0:C, :], bank[7][0:C, 0:C]).then_inc(wkT_ok, 1)
            act.wait_ge(b1_t, 1)
            nc.scalar.copy(b1_sb[:, :], bank[6][:, 0:E * FC]).then_inc(b1_ok, 1)
            for i in range(2):
                act.wait_ge(ctx_t, i + 1)
                nc.scalar.copy(ctxT[0:C, i * 512:i * 512 + 512], bank[i][0:C, :]).then_inc(ctxT_ok, 1)
            for i in range(2):
                act.wait_ge(kv_mm, i + 1)
                nc.scalar.copy(kvT[:, i * 512:i * 512 + 512], bank[2 + i][0:C, :]).then_inc(kv_ok, 1)
            act.wait_ge(kv_mm, 3)
            nc.scalar.copy(kv[:, :, :].rearrange("p t c -> p (t c)"), bank[4][:, :]).then_inc(kv_ok, 1)

            def x2T_copy(b):
                act.wait_ge(x2_t, b + 1)
                if b >= 1:
                    act.wait_ge(lg_mm, b)
                nc.scalar.copy(x2T[:, :, :].rearrange("p c s -> p (c s)"), bank[3][:, :]).then_inc(x2T_ok, 1)

            def normalise(b):
                act.wait_ge(rstd2_ok, b + 1)
                for h in range(HB):
                    i = HB * b + h
                    nc.scalar.activation(sim[:, b % 2, h, :], bank[4 + h][:, 0:S], ACT.Identity,
                                         bias=mrs[:, i:i + 1], scale=nrs[:, i:i + 1]).then_inc(simn_ok, 1)

            def outT_copy(b):
                act.wait_ge(out_mm, b + 1)
                if b >= 1:
                    act.wait_ge(sim_mm, b)
                nc.scalar.mul(outT[:, :], bank[2][0:C, 0:S], float(D) ** -0.5).then_inc(outT_ok, 1)

            def exponentials(b):
                for h in range(HB):
                    i = HB * b + h
                    act.wait_ge(aff_ok, i + 1)
                    nc.scalar.activation(sim[:, b % 2, h, :], sim[:, b % 2, h, :], ACT.Exp,
                                         bias=negmax[:, i:i + 1], scale=-1.0,
                                         accum_out=esum[:, i:i + 1]).then_inc(exp_ok, 1)

            def second_exp(b):
                t = slice(HB * b, HB * b + HB)
                act.wait_ge(dif_ok, b + 1)
                nc.scalar.activation(e2[:, t], dif[:, t], ACT.Exp).then_inc(e2_ok, 1)

            def combT_copy(b):
                act.wait_ge(comb_t, b + 1)
                if b >= 1:
                    act.wait_ge(b2_mm, b)
                nc.scalar.copy(combT[:, :], bank[1][0:E, 0:HB * P]).then_inc(combT_ok, 1)

            def pT_copy(b):
                act.wait_ge(p_t, b + 1)
                if b >= 1:
                    act.wait_ge(out_mm, b)
                nc.scalar.copy(pT[:, :, :].rearrange("p c s -> p (c s)"), bank[0][:, :]).then_inc(pT_ok, 1)

            def high_part(n, q):
                if q == 0:
                    act.wait_ge(w_in[n % STG], 16 * (n // STG + 1))
                r = slice(q * CH // 4, (q + 1) * CH // 4)
                nc.scalar.activation(whi[:, n // 2, n % 2, r], w_stage(n)[:, r], ACT.Copy,
                                     scale=W_SCALE).then_inc(hi_ok, 1)

            def high_half(n):
                for q in range(4):
                    high_part(n, q)

            def store_normed(b):
                act.wait_ge(xn2_ok, HB * (b + 1))
                act.dma_start(xn_rows[b * S:b * S + S, :].rearrange("(h p) d -> p h d", p=P),
                              xn[:, HB * b:HB * b + HB, :]).then_inc(rows_out, 16)

            def store_residual(b):
                act.wait_ge(res_ok, b + 1)
                act.dma_start(out[b * S:b * S + S, :].rearrange("(h p) d -> p h d", p=P),
                              xs[:, HB * b:HB * b + HB, :]).then_inc(res_out, 16)

            for s in range(STEPS):
                if 0 <= s - 4 < B:
                    store_residual(s - 4)
                if 0 <= s - 3 < B:
                    store_normed(s - 3)
                    x2T_copy(s - 3)
                if 0 <= s - 2 < B:
                    normalise(s - 2)
                if 0 <= s - 1 < B:
                    outT_copy(s - 1)
                if 0 <= s - 3 < B:
                    second_exp(s - 3)
                if 0 <= s - 2 < B:
                    exponentials(s - 2)
                if 0 <= s - 3 < B:
                    combT_copy(s - 3)
                if s < B:
                    pT_copy(s)
                if s < EARLY:
                    high_half(s)
            store_residual(B - 1)
            act.wait_ge(b1_ok, 1)
            act.wait_ge(plan_ok, 1)
            act.wait_ge(rows_out, 16 * B)
            act.wait_ge(meta_in, 16)
            total = act.value_load(cendi[0:1, E - 1:E], min_val=16, max_val=MAXT)
            nc.scalar.preload_act_table(ACT.Gelu_apprx_tanh)
            tile = act.alloc_register("act_tile")
            act.reg_mov(tile, 0)

            def token_high(n):
                act.wait_ge(xg_t, n)
                nc.scalar.activation(xhi[:, :, :].rearrange("p c t -> p (c t)"), bank[5][:, 0:D], ACT.Copy,
                                     scale=X_SCALE).then_inc(xhi_ok, 1)

            def expert_tile(e, chunk):
                g = act.snap(tile, min_val=0, max_val=MAXT - 1)
                col = act.value_load(coli[0:1, bass.ds(g, 1)], min_val=0, max_val=E * JT - 1)
                for q in range(FC // 2):
                    act.wait_ge(h_mm, g * 4 + q + 1)
                    for r in range(2):
                        f = 2 * q + r
                        nc.scalar.activation(hact[:, f, :], bank[q][:, r * P:r * P + P], ACT.Gelu_apprx_tanh,
                                             bias=b1_sb[:, e * FC + f:e * FC + f + 1],
                                             scale=1.0 / (X_SCALE * W_SCALE)).then_inc(act_ok, 1)
                    if chunk is not None:
                        high_part(chunk, q)
                with act.If(g + 1 < total):
                    token_high(g + 2)
                act.wait_ge(y_mm, g + 1)
                act.wait_ge(ysb_free, g + 1)
                nc.scalar.activation(ysb[:, :], bank[4][:, 0:D], ACT.Copy,
                                     scale=meta[:, bass.ds(col, 1), 1:2].rearrange("p a b -> p (a b)").bitcast(F32)
                                     ).then_inc(y_ok, 1)
                act.reg_add(tile, tile, 1)

            act.sem_inc(y_ok, 1)
            token_high(1)
            for e in range(E):
                tiles_e = act.value_load(ntile[0:1, e:e + 1], min_val=0, max_val=JT)
                peeled = 2 if 2 * e + EARLY < NW else 0
                for j in range(peeled):
                    with act.If(tiles_e > j):
                        expert_tile(e, 2 * e + EARLY + j)
                    with act.Else():
                        high_half(2 * e + EARLY + j)
                with act.Fori(peeled, JT) as j:
                    with act.If(tiles_e > j):
                        expert_tile(e, None)

        @block.gpsimd
        def _(pool):
            pg = nc.gpsimd
            steps = [0]

            def link(ins):
                steps[0] += 1
                ins.then_inc(pool_step, 1)
                pool.wait_ge(pool_step, steps[0])

            pg.memset(halfneg[:, :], -0.5).then_inc(consts, 1)
            link(pg.memset(ident[:, :], 0.0))
            pg.affine_select(out=ident[:, :], in_=ident[:, :], compare_op=ALU.not_equal, fill=1.0, base=0,
                             pattern=[[-1, P]], channel_multiplier=1).then_inc(consts, 1)
            link(pg.memset(ones[:, :], 1.0))
            pg.affine_select(out=before[:, :], in_=ones[:, :], compare_op=ALU.is_gt, fill=0.0, base=0,
                             pattern=[[1, P]], channel_multiplier=-1).then_inc(consts, 1)
            pg.memset(zeros[:, :], 0.0).then_inc(consts, 1)
            pg.iota(iota_e[:, :], [[1, E]], base=0, channel_multiplier=0,
                    allow_small_or_imprecise_dtypes=True).then_inc(consts, 1)
            pg.iota(giota[:, :], [[1, MAXT + 2]], base=0, channel_multiplier=0,
                    allow_small_or_imprecise_dtypes=True).then_inc(consts, 1)
            for k in range(KTOP):
                pg.iota(entry[:, :, k, 0:1], [[P, TT], [1, 1]], base=0, channel_multiplier=1).then_inc(consts, 1)
            link(pg.memset(meta[:, :, :], 0))
            link(pg.iota(meta[:, :, 0:1], [[0, E * JT], [1, 1]], base=N, channel_multiplier=1))
            pool.wait_ge(consts, 9)
            pool.dma_start(table.rearrange("(p c) k -> p c k", p=P), meta[:, :, :]).then_inc(pads_out, 16)
            pool.dma_start(xn_rows[N:N + PAD, :], zeros[:, :]).then_inc(pads_out, 16)
            pool.dma_start(out[N:N + PAD, :], zeros[:, :]).then_inc(pads_out, 16)

            def inverse_deviation(k, b, eps):
                t = slice(HB * b, HB * b + HB)
                link(pg.tensor_scalar(veps[:, k, t], mv[:, k, t, 1], eps, None, ALU.add))
                return pg.tensor_tensor(rstd[:, k, t], veps[:, k, t], halfneg[:, 0:HB], ALU.pow)

            def low_half(n):
                pool.wait_ge(w_in[n % STG], 16 * (n // STG + 1))
                for q in range(4):
                    r = slice(q * CH // 4, (q + 1) * CH // 4)
                    pool.wait_ge(hi_ok, 4 * n + q + 1)
                    link(pg.tensor_scalar(w_stage(n)[:, r], w_stage(n)[:, r], W_SCALE, 0.0, ALU.mult, ALU.add))
                    pg.tensor_tensor(wlo[:, n // 2, n % 2, r], w_stage(n)[:, r], whi[:, n // 2, n % 2, r],
                                     ALU.subtract).then_inc(lo_ok, 1)

            for b in range(B):
                pool.wait_ge(mv1_ok, HB * (b + 1))
                inverse_deviation(0, b, LN_EPS).then_inc(rstd1_ok, 1)
            for s in range(STEPS):
                if 0 <= s - 1 < B:
                    b = s - 1
                    t = slice(HB * b, HB * b + HB)
                    pool.wait_ge(mv2_ok, HB * (b + 1))
                    link(inverse_deviation(1, b, SIM_EPS))
                    pg.tensor_tensor(mrs[:, t], mv[:, 1, t, 0], rstd[:, 1, t], ALU.mult).then_inc(pool_step, 1)
                    steps[0] += 1
                    link(pg.tensor_scalar(nrs[:, t], rstd[:, 1, t], -1.0, 0.0, ALU.mult, ALU.add))
                    pg.engine_nop().then_inc(rstd2_ok, 1)
                if 0 <= s - 2 < B:
                    b = s - 2
                    pool.wait_ge(mv3_ok, HB * (b + 1))
                    inverse_deviation(2, b, LN_EPS).then_inc(rstd3_ok, 1)
                if 0 <= s - 3 < B:
                    b = s - 3
                    pool.wait_ge(slot_ok, b + 1)
                    if b == 0:
                        pool.wait_ge(pads_out, 48)
                    for i in range(HB * b, HB * b + HB):
                        for k in range(KTOP):
                            pool.indirect_dma_start(
                                out=table, out_offset=bass.IndirectOffsetOnAxis(slot[:, i, k:k + 1].bitcast(U32), 0),
                                in_=entry[:, i, k, :], in_offset=None).then_inc(entry_out, 16)
                if s < EARLY:
                    low_half(s)
            pool.wait_ge(plan_ok, 1)
            pool.wait_ge(meta_in, 16)
            pool.wait_ge(rows_out, 16 * B)
            pool.wait_ge(res_out, 16 * B)
            total = pool.value_load(cendi[0:1, E - 1:E], min_val=16, max_val=MAXT)


            def gather(g, first=False):
                col = pool.value_load(coli[0:1, bass.ds(g, 1)], min_val=0, max_val=E * JT - 1)
                if not first:
                    pool.wait_ge(xg_t, g)
                pg.tensor_copy(gidx[:, :], meta[:, bass.ds(col, 1), 0:1].rearrange("p a b -> p (a b)")
                               ).then_inc(gidx_ok, 1)
                pool.wait_ge(gidx_ok, 1)
                pool.indirect_dma_start(
                    out=xg[:, :], out_offset=None, in_=xn_rows,
                    in_offset=bass.IndirectOffsetOnAxis(gidx[:, :].bitcast(U32), 0)).then_inc(xg_in, 16)
                pool.sem_clear(gidx_ok)

            def add_rows(g, first=False):
                col = pool.value_load(coli[0:1, bass.ds(g, 1)], min_val=0, max_val=E * JT - 1)
                if not first:
                    pool.wait_ge(added, g * 16)
                pool.sem_inc(ysb_free, 1)
                pool.wait_ge(y_ok, g + 2)
                pg.tensor_copy(sidx[:, :], meta[:, bass.ds(col, 1), 0:1].rearrange("p a b -> p (a b)")
                               ).then_inc(sidx_ok, 1)
                pool.wait_ge(sidx_ok, 1)
                pool.indirect_dma_start(
                    out=out, out_offset=bass.IndirectOffsetOnAxis(sidx[:, :].bitcast(U32), 0),
                    in_=ysb[:, :], in_offset=None, compute_op=ALU.add).then_inc(added, 16)
                pool.sem_clear(sidx_ok)

            gather(0, first=True)
            gather(1)
            gather(2)
            add_rows(0, first=True)
            with pool.Fori(1, MAXT) as g:
                with pool.If(g + 2 < total):
                    gather(g + 2)
                with pool.If(g < total):
                    add_rows(g)
            pool.wait_ge(added, total * 16)

        @block.vector
        def _(dve):
            v = nc.vector
            steps = [0]

            def link(ins):
                steps[0] += 1
                ins.then_inc(dve_step, 1)
                dve.wait_ge(dve_step, steps[0])

            def mark(ins):
                steps[0] += 1
                ins.then_inc(dve_step, 1)

            v.memset(ctxT[C:C + 1, :], 1.0).then_inc(consts, 1)
            mark(v.memset(msum[:, 0, :], 0.0))
            mark(v.memset(zer8[:, :], 0.0))

            def tiles(b):
                return range(HB * b, HB * b + HB)

            def input_stats(b):
                dve.wait_ge(x_in[b], 16)
                mark(v.bn_stats(st[:, 0, HB * b, :], xs[:, HB * b, :]))
                link(v.bn_stats(st[:, 0, HB * b + 1, :], xs[:, HB * b + 1, :]))
                for i in tiles(b):
                    v.bn_aggr(mv[:, 0, i, :], st[:, 0, i, :]).then_inc(mv1_ok, 1)

            def input_norm(b):
                dve.wait_ge(rstd1_ok, b + 1)
                dve.wait_ge(mv1_ok, HB * (b + 1))
                for i in tiles(b):
                    v.tensor_scalar(xn[:, i, :], xs[:, i, :], mv[:, 0, i, 0:1], rstd[:, 0, i:i + 1],
                                    ALU.subtract, ALU.mult).then_inc(xn1_ok, 1)

            def sim_stats(b):
                for h in range(HB):
                    dve.wait_ge(sim_mm, HB * b + h + 1)
                    mark(v.bn_stats(st[:, 1, HB * b + h, :], bank[4 + h][:, 0:S]))
                dve.wait_ge(dve_step, steps[0])
                for i in tiles(b):
                    v.bn_aggr(mv[:, 1, i, :], st[:, 1, i, :]).then_inc(mv2_ok, 1)

            def affine(b):
                dve.wait_ge(simn_ok, HB * (b + 1))
                link(v.tensor_tensor(sim[:, b % 2, :, :], sim[:, b % 2, :, :],
                                     gamma[:, :].unsqueeze(1).broadcast_to([P, HB, S]), ALU.mult))
                for h in range(HB):
                    i = HB * b + h
                    v.tensor_tensor_reduce(sim[:, b % 2, h, :], sim[:, b % 2, h, :], negbeta[:, :], 1.0, 3.0e38,
                                           ALU.add, ALU.min, negmax[:, i:i + 1]).then_inc(aff_ok, 1)

            def residual(b):
                t = slice(HB * b, HB * b + HB)
                dve.wait_ge(exp_ok, HB * (b + 1))
                link(v.reciprocal(rsum[:, t], esum[:, t]))
                link(v.tensor_scalar(coef[:, t], rsum[:, t], gates[:, 0:1], None, ALU.mult))
                for h in range(HB):
                    i = HB * b + h
                    mark(v.scalar_tensor_tensor(out=xs[:, i, :], in0=sim[:, b % 2, h, :], scalar=coef[:, i:i + 1],
                                                in1=xs[:, i, :], op0=ALU.mult, op1=ALU.add))
                dve.wait_ge(dve_step, steps[0])
                for i in tiles(b):
                    mark(v.bn_stats(st[:, 2, i, :], xs[:, i, :]))
                dve.wait_ge(dve_step, steps[0])
                for i in tiles(b):
                    v.bn_aggr(mv[:, 2, i, :], st[:, 2, i, :]).then_inc(mv3_ok, 1)

            def token_norm(b):
                dve.wait_ge(rstd3_ok, b + 1)
                dve.wait_ge(p_t, b + 1)
                dve.wait_ge(mv3_ok, HB * (b + 1))
                for i in tiles(b):
                    v.tensor_scalar(xn[:, i, :], xs[:, i, :], mv[:, 2, i, 0:1], rstd[:, 2, i:i + 1],
                                    ALU.subtract, ALU.mult).then_inc(xn2_ok, 1)

            def top_two(b):
                t = slice(HB * b, HB * b + HB)
                dve.wait_ge(lg_mm, b + 1)
                link(v.tensor_tensor(lg[:, t, :], bank[6][:, 0:HB * E].rearrange("p (h e) -> p h e", h=HB),
                                     gb[:, :].unsqueeze(1).broadcast_to([P, HB, E]), ALU.add))
                for i in tiles(b):
                    mark(v.max(mx[:, i, :], lg[:, i, :]))
                dve.wait_ge(dve_step, steps[0])
                v.tensor_tensor(dif[:, t], mx[:, t, 1], mx[:, t, 0], ALU.subtract).then_inc(dif_ok, 1)
                for i in tiles(b):
                    mark(v.max_index(ix[:, i, :], mx[:, i, :], lg[:, i, :]))
                dve.wait_ge(dve_step, steps[0])
                link(v.tensor_copy(ixf[:, t, :], ix[:, t, 0:KTOP]))
                link(v.tensor_tensor(mask[:, t, :, :].rearrange("p h k e -> p (h k) e"),
                                     iota_e[:, :].unsqueeze(1).broadcast_to([P, HB * KTOP, E]),
                                     ixf[:, t, :].rearrange("p h k -> p (h k)").unsqueeze(2).broadcast_to(
                                         [P, HB * KTOP, E]), ALU.is_equal))
                link(v.tensor_tensor(mcount[:, t, :], mask[:, t, 0, :], mask[:, t, 1, :], ALU.add))
                link(v.tensor_tensor(msum[:, HB * b + 1, :], msum[:, HB * b, :], mcount[:, HB * b, :], ALU.add))
                v.tensor_tensor(msum[:, HB * b + 2, :], msum[:, HB * b + 1, :], mcount[:, HB * b + 1, :],
                                ALU.add).then_inc(mask_ok, 1)

            def weights(b):
                t = slice(HB * b, HB * b + HB)
                dve.wait_ge(e2_ok, b + 1)
                link(v.tensor_scalar(den[:, t], e2[:, t], 1.0, None, ALU.add))
                link(v.reciprocal(wk2[:, t, 0], den[:, t]))
                link(v.tensor_tensor(wk2[:, t, 1], e2[:, t], wk2[:, t, 0], ALU.mult))
                mark(v.tensor_scalar(entry[:, t, :, 1].bitcast(F32), wk2[:, t, :], gslot[:, 0:1], None, ALU.mult))
                link(v.tensor_tensor(wmask[:, t, :, :].rearrange("p h k e -> p (h k) e"),
                                     mask[:, t, :, :].rearrange("p h k e -> p (h k) e"),
                                     wk2[:, t, :].rearrange("p h k -> p (h k)").unsqueeze(2).broadcast_to(
                                         [P, HB * KTOP, E]), ALU.mult))
                v.tensor_tensor(comb[:, t, :], wmask[:, t, 0, :], wmask[:, t, 1, :], ALU.add).then_inc(comb_ok, 1)

            def slots(b):
                t = slice(HB * b, HB * b + HB)
                dve.wait_ge(rank_mm, b + 1)
                for k in range(KTOP):
                    mark(v.tensor_tensor(rmask[:, t, k, :], bank[7][:, 0:HB * E].rearrange("p (h e) -> p h e", h=HB),
                                         mask[:, t, k, :], ALU.mult))
                dve.wait_ge(dve_step, steps[0])
                link(v.tensor_reduce(rankf[:, t, :], rmask[:, t, :, :], mybir.AxisListType.X, ALU.add))
                link(v.tensor_copy(ranki[:, t, :], rankf[:, t, :]))
                link(v.tensor_scalar(rlow[:, t, :], ranki[:, t, :], P - 1, 6, ALU.bitwise_and, ALU.logical_shift_left))
                link(v.scalar_tensor_tensor(out=rrow[:, t, :], in0=ranki[:, t, :], scalar=7, in1=rlow[:, t, :],
                                            op0=ALU.logical_shift_right, op1=ALU.bitwise_or))
                v.scalar_tensor_tensor(out=slot[:, t, :], in0=ix[:, t, 0:KTOP].bitcast(I32), scalar=3,
                                       in1=rrow[:, t, :], op0=ALU.logical_shift_left,
                                       op1=ALU.bitwise_or).then_inc(slot_ok, 1)

            def bias_out(b):
                t = slice(HB * b, HB * b + HB)
                dve.wait_ge(b2_mm, b + 1)
                v.scalar_tensor_tensor(out=xs[:, t, :].rearrange("p h d -> p (h d)"), in0=bank[1][:, :],
                                       scalar=gates[:, 1:2], in1=xs[:, t, :].rearrange("p h d -> p (h d)"),
                                       op0=ALU.mult, op1=ALU.add).then_inc(res_ok, 1)

            for b in range(B):
                input_stats(b)
                if b >= 1:
                    input_norm(b - 1)
            dve.wait_ge(tanh_ok, 1)
            mark(v.tensor_scalar(negbeta[:, :], negbeta[:, :], -1.0, None, ALU.mult))
            mark(v.tensor_scalar(gslot[:, :], gates[:, 1:2], 1.0 / (H_SCALE * W_SCALE), None, ALU.mult))
            input_norm(B - 1)
            dve.wait_ge(dve_step, steps[0])
            for s in range(1, STEPS):
                if 0 <= s - 3 < B:
                    token_norm(s - 3)
                if 0 <= s - 2 < B:
                    affine(s - 2)
                if 0 <= s - 3 < B:
                    top_two(s - 3)
                if 0 <= s - 1 < B:
                    sim_stats(s - 1)
                if 0 <= s - 3 < B:
                    weights(s - 3)
                if 0 <= s - 2 < B:
                    residual(s - 2)
                if 0 <= s - 3 < B:
                    slots(s - 3)
                    bias_out(s - 3)

            dve.wait_ge(cnt_mm, 1)
            link(v.tensor_copy(cnti[:, :], bank[7][0:1, 64:64 + E]))
            link(v.tensor_scalar(cntr[:, :], cnti[:, :], P - 1, None, ALU.add))
            link(v.tensor_scalar(ntile[:, :], cntr[:, :], 7, None, ALU.logical_shift_right))
            link(v.tensor_copy(ntf[:, :], ntile[:, :]))
            link(v.tensor_tensor_scan(cend[:, :], ntf[:, :], zer8[:, :], 0.0, ALU.add, ALU.add))
            mark(v.tensor_copy(cendi[:, :], cend[:, :]))
            link(v.tensor_tensor(past[:, :, :], cend[:, :].unsqueeze(1).broadcast_to([1, MAXT + 2, E]),
                                 giota[:, :].unsqueeze(2).broadcast_to([1, MAXT + 2, E]), ALU.is_le))
            mark(v.tensor_tensor(pastn[:, :, :], past[:, :, :], ntf[:, :].unsqueeze(1).broadcast_to([1, MAXT + 2, E]),
                                 ALU.mult))
            link(v.tensor_reduce(eg[:, :], past[:, :, :], mybir.AxisListType.X, ALU.add))
            mark(v.tensor_scalar(egi[:, :], eg[:, :], float(FC), None, ALU.mult))
            link(v.tensor_reduce(sg[:, :], pastn[:, :, :], mybir.AxisListType.X, ALU.add))
            link(v.tensor_tensor(col1[:, :], giota[:, :], sg[:, :], ALU.subtract))
            link(v.scalar_tensor_tensor(out=col2[:, :], in0=eg[:, :], scalar=float(JT), in1=col1[:, :],
                                        op0=ALU.mult, op1=ALU.add))
            v.tensor_copy(coli[:, :], col2[:, :]).then_inc(plan_ok, 1)

            def low_part(n, q):
                if q == 0:
                    dve.wait_ge(w_in[n % STG], 16 * (n // STG + 1))
                r = slice(q * CH // 4, (q + 1) * CH // 4)
                dve.wait_ge(hi_ok, 4 * n + q + 1)
                v.scalar_tensor_tensor(out=wlo[:, n // 2, n % 2, r], in0=w_stage(n)[:, r], scalar=W_SCALE,
                                       in1=whi[:, n // 2, n % 2, r], op0=ALU.mult,
                                       op1=ALU.subtract).then_inc(lo_ok, 1)

            def token_low(n):
                dve.wait_ge(xhi_ok, n)
                v.scalar_tensor_tensor(out=xlo[:, :, :].rearrange("p c t -> p (c t)"), in0=bank[5][:, 0:D],
                                       scalar=X_SCALE, in1=xhi[:, :, :].rearrange("p c t -> p (c t)"),
                                       op0=ALU.mult, op1=ALU.subtract).then_inc(xlo_ok, 1)

            def expert_tile(chunk):
                g = dve.snap(tile, min_val=0, max_val=MAXT - 1)
                for q in range(FC // 2):
                    f = slice(2 * q, 2 * q + 2)
                    dve.wait_ge(act_ok, g * FC + 2 * q + 2)
                    v.tensor_scalar(hhi[:, f, :], hact[:, f, :], H_SCALE, None, ALU.mult).then_inc(hhi_ok, 1)
                    dve.wait_ge(hhi_ok, g * 4 + q + 1)
                    v.scalar_tensor_tensor(out=hlo[:, f, :], in0=hact[:, f, :], scalar=H_SCALE,
                                           in1=hhi[:, f, :], op0=ALU.mult, op1=ALU.subtract).then_inc(hsplit_ok, 1)
                    if chunk is not None:
                        low_part(chunk, q)
                with dve.If(g + 1 < total):
                    token_low(g + 2)
                dve.reg_add(tile, tile, 1)

            dve.wait_ge(plan_ok, 1)
            total = dve.value_load(cendi[0:1, E - 1:E], min_val=16, max_val=MAXT)
            tile = dve.alloc_register("dve_tile")
            dve.reg_mov(tile, 0)
            token_low(1)
            for e in range(E):
                tiles_e = dve.value_load(ntile[0:1, e:e + 1], min_val=0, max_val=JT)
                peeled = 2 if 2 * e + EARLY < NW else 0
                for j in range(peeled):
                    with dve.If(tiles_e > j):
                        expert_tile(2 * e + EARLY + j)
                    with dve.Else():
                        for q in range(4):
                            low_part(2 * e + EARLY + j, q)
                with dve.Fori(peeled, JT) as j:
                    with dve.If(tiles_e > j):
                        expert_tile(None)

        @block.tensor
        def _(pe):
            pe.wait_ge(consts, 9)
            pe.wait_ge(small_in, 16 * NSMALL)
            pe.transpose(bank[7][0:C, 0:C], wk_sb[:, :], ident[0:C, 0:C]).then_inc(wk_t, 1)
            pe.transpose(bank[6][:, 0:E * FC], b1_rows[:, :], ident[0:E * FC, 0:E * FC]).then_inc(b1_t, 1)
            pe.wait_ge(ctx_in, 16)
            for i in range(TT):
                t = pe.transpose(bank[i // 4][0:C, i % 4 * P:i % 4 * P + P], ctx_sb[:, i, :], ident[:, :])
                if i % 4 == 3:
                    t.then_inc(ctx_t, 1)
            pe.wait_ge(wkT_ok, 1)
            for i in range(2):
                pe.wait_ge(ctxT_ok, i + 1)
                pe.matmul(bank[2 + i][0:C, :], wkT[:, :], ctxT[:, i * 512:i * 512 + 512],
                          start=True, stop=True).then_inc(kv_mm, 1)
            for i in range(TT):
                m = pe.matmul(bank[4][:, i * C:i * C + C], ctxT[:, i * P:i * P + P], wkT[:, :], start=True, stop=True)
            m.then_inc(kv_mm, 1)

            def transpose_p(b):
                pe.wait_ge(xn1_ok, HB * (b + 1))
                if b == 0:
                    pe.wait_ge(ctxT_ok, 1)
                else:
                    pe.wait_ge(pT_ok, b)
                for h in range(HB):
                    for c in range(DC):
                        t = pe.transpose(bank[0][:, c * S + h * P:c * S + h * P + P],
                                         xn[:, HB * b + h, c * P:c * P + P], ident[:, :])
                t.then_inc(p_t, 1)

            def attend(b):
                pe.wait_ge(pT_ok, b + 1)
                pe.wait_ge(kv_ok, 3)
                if b >= 1:
                    pe.wait_ge(outT_ok, b)
                for c in range(DC):
                    m = pe.matmul(bank[2][0:C, 0:S], kv[:, HB * b + c, :], pT[:, c, :],
                                  start=(c == 0), stop=(c == DC - 1))
                m.then_inc(out_mm, 1)

            def similarities(b):
                pe.wait_ge(outT_ok, b + 1)
                if b >= 1:
                    pe.wait_ge(simn_ok, HB * b)
                for h in range(HB):
                    pe.matmul(bank[4 + h][:, 0:S], outT[:, h * P:h * P + P], kvT[:, b * S:b * S + S],
                              start=True, stop=True).then_inc(sim_mm, 1)

            def logits(b):
                pe.wait_ge(xn2_ok, HB * (b + 1))
                if b >= 1:
                    pe.wait_ge(x2T_ok, b)
                for h in range(HB):
                    for c in range(DC):
                        t = pe.transpose(bank[3][:, c * S + h * P:c * S + h * P + P],
                                         xn[:, HB * b + h, c * P:c * P + P], ident[:, :])
                t.then_inc(x2_t, 1)
                pe.wait_ge(x2T_ok, b + 1)
                if b == 0:
                    pe.wait_ge(b1_ok, 1)
                else:
                    pe.wait_ge(mask_ok, b)
                for h in range(HB):
                    for c in range(DC):
                        m = pe.matmul(bank[6][:, h * E:h * E + E], x2T[:, c, h * P:h * P + P], gw[:, c, :],
                                      start=(c == 0), stop=(c == DC - 1))
                m.then_inc(lg_mm, 1)

            def ranks(b):
                pe.wait_ge(mask_ok, b + 1)
                if b >= 1:
                    pe.wait_ge(slot_ok, b)
                for h in range(HB):
                    i = HB * b + h
                    o = bank[7][:, h * E:h * E + E]
                    pe.matmul(o, before[:, :], mcount[:, i, :], start=True, stop=False)
                    m = pe.matmul(o, ones[:, :], msum[:, i, :], start=False, stop=True)
                m.then_inc(rank_mm, 1)

            def bias_rows(b):
                pe.wait_ge(comb_ok, b + 1)
                pe.wait_ge(ctxT_ok, 2)
                if b >= 1:
                    pe.wait_ge(res_ok, b)
                for h in range(HB):
                    t = pe.transpose(bank[1][0:E, h * P:h * P + P], comb[:, HB * b + h, :], ident[:, :])
                t.then_inc(comb_t, 1)
                pe.wait_ge(combT_ok, b + 1)
                for h in range(HB):
                    m = pe.matmul(bank[1][:, h * D:h * D + D], combT[:, h * P:h * P + P], b2_sb[:, :],
                                  start=True, stop=True)
                m.then_inc(b2_mm, 1)

            for s in range(STEPS):
                if 0 <= s - 3 < B:
                    logits(s - 3)
                if 0 <= s - 1 < B:
                    attend(s - 1)
                    similarities(s - 1)
                if 0 <= s - 3 < B:
                    ranks(s - 3)
                    bias_rows(s - 3)
                if s < B:
                    transpose_p(s)
            pe.wait_ge(slot_ok, B)
            pe.matmul(bank[7][:, 64:64 + E], ones[:, :], msum[:, TT, :], start=True, stop=True).then_inc(cnt_mm, 1)

            pe.wait_ge(plan_ok, 1)
            pe.wait_ge(res_ok, B)
            pe.wait_ge(rstd3_ok, B)
            tile = pe.alloc_register("pe_tile")
            pe.reg_mov(tile, 0)
            total = pe.value_load(cendi[0:1, E - 1:E], min_val=16, max_val=MAXT)

            def transpose_tokens(n):
                pe.wait_ge(xg_in, n * 16)
                for c in range(DC):
                    t = pe.transpose(bank[5][:, c * P:c * P + P], xg[:, c * P:c * P + P], ident[:, :])
                t.then_inc(xg_t, 1)

            transpose_tokens(1)
            for e in range(E):
                tiles_e = pe.value_load(ntile[0:1, e:e + 1], min_val=0, max_val=JT)
                with pe.Fori(0, JT) as j:
                    with pe.If(j < tiles_e):
                        g = pe.snap(tile, min_val=0, max_val=MAXT - 1)
                        pe.wait_ge(hi_ok, 8 * e + 8)
                        pe.wait_ge(lo_ok, 8 * e + 8)
                        pe.wait_ge(xlo_ok, g + 1)
                        for q in range(FC // 2):
                            for r in range(2):
                                f = 2 * q + r
                                k = 0
                                for c in range(DC):
                                    w = slice(c * F + f * P, c * F + f * P + P)
                                    for wt, xt in ((whi, xhi), (whi, xlo), (wlo, xhi)):
                                        m = pe.matmul(bank[q][:, r * P:r * P + P], wt[:, e, 0, w], xt[:, c, :],
                                                      start=(k == 0), stop=(k == 3 * DC - 1))
                                        k += 1
                            m.then_inc(h_mm, 1)
                        with pe.If(g + 1 < total):
                            transpose_tokens(g + 2)
                        pe.wait_ge(y_ok, g + 1)
                        for f in range(FC):
                            if f % 2 == 0:
                                pe.wait_ge(hsplit_ok, g * 4 + f // 2 + 1)
                            for ht, wt in ((hhi, whi), (hhi, wlo), (hlo, whi)):
                                m = pe.matmul(bank[4][:, 0:D], ht[:, f, :], wt[:, e, 1, f * D:f * D + D],
                                              start=(f == 0 and ht is hhi and wt is whi),
                                              stop=(f == FC - 1 and ht is hlo))
                        m.then_inc(y_mm, 1)
                        pe.reg_add(tile, tile, 1)


_INS = ['x', 'ctx_512', 'g_xattn', 'g_ffn', 'L0_xattn_W_k', 'L0_xattn_b_k', 'L0_xattn_ln_gamma', 'L0_xattn_ln_beta',
        'L0_ffn_gate_w', 'L0_ffn_gate_b', 'L0_ffn_w1', 'L0_ffn_b1', 'L0_ffn_w2', 'L0_ffn_b2']


def kernel(**inputs):
    import numpy as _np
    import concourse.bacc as _bacc
    from concourse import mybir as _mybir
    from concourse.bass_utils import run_bass_kernel_spmd as _run

    nc = _bacc.Bacc("TRN2", target_bir_lowering=False, num_devices=1)
    arrays, args = {}, []
    for name in _INS:
        a = _np.ascontiguousarray(inputs[name])
        arrays[f"in_{name}"] = a
        args.append(nc.dram_tensor(f"in_{name}", a.shape, _mybir.dt.from_np(a.dtype), kind="ExternalInput").ap())
    B, S, D = inputs['x'].shape
    out = nc.dram_tensor("out_rows", (B * S + 128, D), _mybir.dt.float32, kind="ExternalOutput").ap()
    gated_block(nc, *args, out)
    r = _run(nc, [arrays], core_ids=[0])
    return r.results[0]["out_rows"][:B * S].reshape(B, S, D)
```

```python
from contextlib import ExitStack

import numpy as np

import concourse.bass as bass
from concourse import mybir

ALU = mybir.AluOpType
ACT = mybir.ActivationFunctionType
F32 = mybir.dt.float32
F16 = mybir.dt.float16
BF16 = mybir.dt.bfloat16
I32 = mybir.dt.int32
U32 = mybir.dt.uint32
P = 128

X_SCALE = 2.0 ** 10
W_SCALE = 2.0 ** 10
H_SCALE = 2.0 ** 6
LN_EPS = 1e-5
SIM_EPS = 1e-6


def gated_block(nc, x, ctx_kv, g_xattn, g_ffn, w_k, b_k, ln_gamma, ln_beta,
                gate_w, gate_b, w1, b1, w2, b2, out):
    B, S, D = x.shape
    C = ctx_kv.shape[2]
    E, _, F = w1.shape
    N = B * S
    TT = N // P
    HB = S // P
    DC = D // P
    FC = F // P
    KTOP = 2
    JT = N // P
    SLOTS = E * N
    MAXT = (KTOP * N + E * (P - 1)) // P
    PAD = P
    STG = 3
    CH = DC * F
    assert DC * F == FC * D and S == D and HB == 2 and DC == 2 and FC == 8 and E == 8

    xn_rows = nc.dram_tensor("xn_rows", (N + PAD, D), F32).ap()
    table = nc.dram_tensor("table", (SLOTS, 2), I32).ap()

    es = ExitStack()
    with es:
        def sb(name, shape, dt):
            return es.enter_context(nc.sbuf_tensor(name, shape, dt))

        def sem(name):
            return es.enter_context(nc.semaphore(name))

        bank = [es.enter_context(nc.psum_tensor(f"bank{i}", [P, 512], F32)) for i in range(8)]

        whi = sb("whi", [P, E, 2, CH], F16)
        wlo = sb("wlo", [P, E, 2, CH], F16)
        stage = sb("stage", [P, STG, CH], F32)
        xs = sb("xs", [P, TT, D], F32)
        xn = sb("xn", [P, TT, D], F32)
        ctx_sb = sb("ctx_sb", [P, TT, C], F32)
        ctxT = sb("ctxT", [C + 1, N], F32)
        wk_sb = sb("wk_sb", [C, C], F32)
        wkT = sb("wkT", [C + 1, C], F32)
        kvT = sb("kvT", [C, N], F32)
        kv = sb("kv", [P, TT, C], F32)
        pT = sb("pT", [P, DC, S], F32)
        outT = sb("outT", [C, S], F32)
        sim = sb("sim", [P, 2, HB, S], F32)
        negbeta = sb("negbeta", [P, S], F32)
        neggamma = sb("neggamma", [P, S], F32)
        x2T = sb("x2T", [P, DC, S], F32)
        gw = sb("gw", [P, DC, E], F32)
        gb = sb("gb", [P, E], F32)
        b2_sb = sb("b2_sb", [E, D], F32)
        b1_rows = sb("b1_rows", [E * FC, P], F32)
        b1_sb = sb("b1_sb", [P, E * FC], F32)
        gates = sb("gates", [P, 2], F32)
        gslot = sb("gslot", [P, 1], F32)
        ident = sb("ident", [P, P], F32)
        before = sb("before", [P, P], BF16)
        ones = sb("ones", [P, P], BF16)
        zeros = sb("zeros", [P, D], F32)
        halfneg = sb("halfneg", [P, 8], F32)
        st = sb("st", [P, 3, TT, 6], F32)
        mv = sb("mv", [P, 3, TT, 2], F32)
        veps = sb("veps", [P, 3, TT], F32)
        rstd = sb("rstd", [P, 3, TT], F32)
        mneg = sb("mneg", [P, 3, TT], F32)
        nmr = sb("nmr", [P, TT], F32)
        negmax = sb("negmax", [P, TT], F32)
        esum = sb("esum", [P, TT], F32)
        rsum = sb("rsum", [P, TT], F32)
        coef = sb("coef", [P, TT], F32)
        lg = sb("lg", [P, TT, E], F32)
        mx = sb("mx", [P, TT, 8], F32)
        ix = sb("ix", [P, TT, 8], U32)
        ixf = sb("ixf", [P, TT, KTOP], F32)
        iota_e = sb("iota_e", [P, E], F32)
        dif = sb("dif", [P, TT], F32)
        e2 = sb("e2", [P, TT], F32)
        den = sb("den", [P, TT], F32)
        wk2 = sb("wk2", [P, TT, KTOP], F32)
        mask = sb("mask", [P, TT, KTOP, E], F32)
        mcount = sb("mcount", [P, TT, E], BF16)
        wmask = sb("wmask", [P, TT, KTOP, E], F32)
        comb = sb("comb", [P, TT, E], F32)
        combT = sb("combT", [E, HB * P], F32)
        rmask = sb("rmask", [P, TT, KTOP, E], F32)
        ranki = sb("ranki", [P, TT, KTOP], I32)
        rlow = sb("rlow", [P, TT, KTOP], I32)
        rrow = sb("rrow", [P, TT, KTOP], I32)
        slot = sb("slot", [P, TT, KTOP], I32)
        entry = sb("entry", [P, TT, KTOP, 2], I32)
        meta = sb("meta", [P, E * JT, 2], I32)
        cnti = sb("cnti", [1, E], I32)
        cntr = sb("cntr", [1, E], I32)
        ntile = sb("ntile", [1, E], I32)
        ntf = sb("ntf", [1, E], F32)
        zer8 = sb("zer8", [1, E], F32)
        cend = sb("cend", [1, E], F32)
        cendi = sb("cendi", [1, E], I32)
        giota = sb("giota", [1, MAXT + 2], F32)
        past = sb("past", [1, MAXT + 2, E], F32)
        pastn = sb("pastn", [1, MAXT + 2, E], F32)
        eg = sb("eg", [1, MAXT + 2], F32)
        sg = sb("sg", [1, MAXT + 2], F32)
        col1 = sb("col1", [1, MAXT + 2], F32)
        col2 = sb("col2", [1, MAXT + 2], F32)
        coli = sb("coli", [1, MAXT + 2], I32)
        egi = sb("egi", [1, MAXT + 2], I32)
        gidx = sb("gidx", [P, 1], I32)
        sidx = sb("sidx", [P, 1], I32)
        wcur = sb("wcur", [P, 1], I32)
        xhi = sb("xhi", [P, DC, P], F16)
        xlo = sb("xlo", [P, DC, P], F16)
        hact = xn[:, 0:4, :].rearrange("p a b -> p (a b)").rearrange("p (f t) -> p f t", f=FC)
        hhi = xn[:, 4:6, :].bitcast(F16).rearrange("p a b -> p (a b)").rearrange("p (f t) -> p f t", f=FC)
        hlo = xn[:, 6:8, :].bitcast(F16).rearrange("p a b -> p (a b)").rearrange("p (f t) -> p f t", f=FC)
        xg = ctx_sb[:, 0:4, :].rearrange("p a b -> p (a b)")
        ysb = ctx_sb[:, 4:8, :].rearrange("p a b -> p (a b)")

        x_in = [sem(f"x_in{b}") for b in range(B)]
        ctx_in = sem("ctx_in")
        small_in = sem("small_in")
        pads_out = sem("pads_out")
        w_in = [sem(f"w_in{i}") for i in range(STG)]
        consts = sem("consts")
        wk_t = sem("wk_t")
        wkT_ok = sem("wkT_ok")
        b1_t = sem("b1_t")
        b1_ok = sem("b1_ok")
        ctx_t = sem("ctx_t")
        ctxT_ok = sem("ctxT_ok")
        kv_mm = sem("kv_mm")
        kv_ok = sem("kv_ok")
        kvT_mm = sem("kvT_mm")
        kvT_ok = sem("kvT_ok")
        gate_in = sem("gate_in")
        ident_ok = sem("ident_ok")
        ones_row = sem("ones_row")
        tanh_ok = sem("tanh_ok")
        dve_step = sem("dve_step")
        pool_step = sem("pool_step")
        mv1_ok = sem("mv1_ok")
        xn1_ok = sem("xn1_ok")
        p_t = sem("p_t")
        pT_ok = sem("pT_ok")
        out_mm = sem("out_mm")
        outT_ok = sem("outT_ok")
        sim_mm = sem("sim_mm")
        mv2_ok = sem("mv2_ok")
        rstd2_ok = sem("rstd2_ok")
        simn_ok = sem("simn_ok")
        aff_ok = sem("aff_ok")
        exp_ok = sem("exp_ok")
        mv3_ok = sem("mv3_ok")
        xn2_ok = sem("xn2_ok")
        rows_out = sem("rows_out")
        x2_t = sem("x2_t")
        x2T_ok = sem("x2T_ok")
        lg_mm = sem("lg_mm")
        dif_ok = sem("dif_ok")
        e2_ok = sem("e2_ok")
        mask_ok = sem("mask_ok")
        rank_mm = sem("rank_mm")
        slot_ok = sem("slot_ok")
        entry_out = sem("entry_out")
        comb_ok = sem("comb_ok")
        comb_t = sem("comb_t")
        combT_ok = sem("combT_ok")
        b2_mm = sem("b2_mm")
        res_ok = sem("res_ok")
        res_out = sem("res_out")
        hi_ok = sem("hi_ok")
        lo_ok = sem("lo_ok")
        cnt_mm = sem("cnt_mm")
        plan_ok = sem("plan_ok")
        meta_in = sem("meta_in")
        gidx_ok = sem("gidx_ok")
        xg_in = sem("xg_in")
        xg_t = sem("xg_t")
        xhi_ok = sem("xhi_ok")
        xlo_ok = sem("xlo_ok")
        h_mm = sem("h_mm")
        act_ok = sem("act_ok")
        hhi_ok = sem("hhi_ok")
        hsplit_ok = sem("hsplit_ok")
        y_mm = sem("y_mm")
        y_ok = sem("y_ok")
        sidx_ok = sem("sidx_ok")
        added = sem("added")
        ysb_free = sem("ysb_free")

        NSMALL = 5
        NCONST = 7
        STEPS = B + 2
        NW = 2 * E
        PEEL = 3
        EARLY = 4

        def w_dram(n):
            e, which = divmod(n, 2)
            src = w2 if which else w1
            return src[e].rearrange("(c p) n -> p c n", p=P)

        def w_stage(n, lo=0, hi=CH):
            return stage[:, n % STG, lo:hi]

        block = es.enter_context(nc.Block())

        @block.sync
        def _(sp):
            sp.dma_start(xs[:, 0:HB, :], x[0].rearrange("(h p) d -> p h d", p=P)).then_inc(x_in[0], 16)
            for b in range(1, B):
                sp.dma_start(xs[:, HB * b:HB * b + HB, :],
                             x[b].rearrange("(h p) d -> p h d", p=P)).then_inc(x_in[b], 16)
            sp.dma_start(gw[:, :, :], gate_w.rearrange("(c p) e -> p c e", p=P)).then_inc(gate_in, 16)
            sp.dma_start(gb[:, :], gate_b.partition_broadcast(P)).then_inc(gate_in, 16)
            sp.dma_start(b2_sb[:, :], b2).then_inc(gate_in, 16)

            def load_weights(n):
                if n >= STG:
                    sp.wait_ge(hi_ok, 4 * (n - STG + 1))
                    sp.wait_ge(lo_ok, 4 * (n - STG + 1))
                c = DC if n % 2 == 0 else FC
                sp.dma_start(w_stage(n).rearrange("p (c n) -> p c n", c=c), w_dram(n)).then_inc(w_in[n % STG], 16)

            for n in range(STG):
                load_weights(n)
            sp.wait_ge(consts, NCONST)
            sp.dma_start(table.rearrange("(p c) k -> p c k", p=P), meta[:, :, :]).then_inc(pads_out, 16)
            sp.dma_start(xn_rows[N:N + PAD, :], zeros[:, :]).then_inc(pads_out, 16)
            sp.dma_start(out[N:N + PAD, :], zeros[:, :]).then_inc(pads_out, 16)
            for n in range(STG, EARLY + 2):
                load_weights(n)
            sp.wait_ge(entry_out, 16 * TT * KTOP)
            sp.dma_start(meta[:, :, :], table.rearrange("(p c) k -> p c k", p=P)).then_inc(meta_in, 16)
            for n in range(EARLY + 2, NW):
                load_weights(n)

        @block.scalar
        def _(act):
            act.dma_start(ctx_sb[:, :, :], ctx_kv.rearrange("b (h p) c -> p (b h) c", p=P)).then_inc(ctx_in, 16)
            act.dma_start(wk_sb[:, :], w_k).then_inc(ctx_in, 16)
            act.dma_start(wkT[C:C + 1, :], b_k.unsqueeze(0)).then_inc(ctx_in, 16)
            act.dma_start(gates[:, 0:1], g_xattn.partition_broadcast(P)).then_inc(small_in, 16)
            act.dma_start(gates[:, 1:2], g_ffn.partition_broadcast(P)).then_inc(small_in, 16)
            act.dma_start(neggamma[:, :], ln_gamma.partition_broadcast(P)).then_inc(small_in, 16)
            act.dma_start(negbeta[:, :], ln_beta.partition_broadcast(P)).then_inc(small_in, 16)
            act.dma_start(b1_rows[:, :], b1.rearrange("e (c p) -> (e c) p", p=P)).then_inc(small_in, 16)

            act.wait_ge(wk_t, 1)
            nc.scalar.copy(wkT[0:C, :], bank[7][0:C, 0:C]).then_inc(wkT_ok, 1)
            for i in range(2):
                act.wait_ge(ctx_t, i + 1)
                nc.scalar.copy(ctxT[0:C, i * 512:i * 512 + 512], bank[i][0:C, :]).then_inc(ctxT_ok, 1)
            act.wait_ge(small_in, 16 * NSMALL)
            nc.scalar.activation(gates[:, :], gates[:, :], ACT.Tanh).then_inc(tanh_ok, 1)

            def kvT_copy(i):
                act.wait_ge(kvT_mm, i + 1)
                nc.scalar.copy(kvT[:, i * 512:i * 512 + 512], bank[2 + i][0:C, :]).then_inc(kvT_ok, 1)

            def x2T_copy(b):
                act.wait_ge(x2_t, b + 1)
                if b >= 1:
                    act.wait_ge(lg_mm, b)
                nc.scalar.copy(x2T[:, :, :].rearrange("p c s -> p (c s)"), bank[3][:, :]).then_inc(x2T_ok, 1)

            def normalise(b):
                act.wait_ge(rstd2_ok, b + 1)
                for h in range(HB):
                    i = HB * b + h
                    nc.scalar.activation(sim[:, b % 2, h, :], bank[4 + h][:, 0:S], ACT.Identity,
                                         bias=nmr[:, i:i + 1], scale=rstd[:, 1, i:i + 1]).then_inc(simn_ok, 1)

            def outT_copy(b):
                act.wait_ge(out_mm, b + 1)
                if b >= 1:
                    act.wait_ge(sim_mm, b)
                nc.scalar.mul(outT[:, :], bank[2][0:C, 0:S], float(D) ** -0.5).then_inc(outT_ok, 1)

            def exponentials(b):
                for h in range(HB):
                    i = HB * b + h
                    act.wait_ge(aff_ok, i + 1)
                    nc.scalar.activation(sim[:, b % 2, h, :], sim[:, b % 2, h, :], ACT.Exp,
                                         bias=negmax[:, i:i + 1], scale=-1.0,
                                         accum_out=esum[:, i:i + 1]).then_inc(exp_ok, 1)

            def second_exp(b):
                t = slice(HB * b, HB * b + HB)
                act.wait_ge(dif_ok, b + 1)
                nc.scalar.activation(e2[:, t], dif[:, t], ACT.Exp).then_inc(e2_ok, 1)

            def combT_copy(b):
                act.wait_ge(comb_t, b + 1)
                if b >= 1:
                    act.wait_ge(b2_mm, b)
                nc.scalar.copy(combT[:, :], bank[1][0:E, 0:HB * P]).then_inc(combT_ok, 1)

            def pT_copy(b):
                act.wait_ge(p_t, b + 1)
                if b >= 1:
                    act.wait_ge(out_mm, b)
                nc.scalar.copy(pT[:, :, :].rearrange("p c s -> p (c s)"), bank[0][:, :]).then_inc(pT_ok, 1)

            def high_part(n, q):
                if q == 0:
                    act.wait_ge(w_in[n % STG], 16 * (n // STG + 1))
                r = slice(q * CH // 4, (q + 1) * CH // 4)
                nc.scalar.activation(whi[:, n // 2, n % 2, r], w_stage(n)[:, r], ACT.Copy,
                                     scale=W_SCALE).then_inc(hi_ok, 1)

            def high_half(n):
                for q in range(4):
                    high_part(n, q)

            def store_normed(b):
                act.wait_ge(xn2_ok, HB * (b + 1))
                act.dma_start(xn_rows[b * S:b * S + S, :].rearrange("(h p) d -> p h d", p=P),
                              xn[:, HB * b:HB * b + HB, :]).then_inc(rows_out, 16)

            def store_residual(b):
                act.wait_ge(res_ok, b + 1)
                act.dma_start(out[b * S:b * S + S, :].rearrange("(h p) d -> p h d", p=P),
                              xs[:, HB * b:HB * b + HB, :]).then_inc(res_out, 16)

            kvT_copy(0)
            act.wait_ge(kv_mm, 1)
            nc.scalar.copy(kv[:, :, :].rearrange("p t c -> p (t c)"), bank[4][:, :]).then_inc(kv_ok, 1)
            pT_copy(0)
            for s in range(STEPS):
                if 0 <= s - 1 < B:
                    normalise(s - 1)
                if 0 <= s - 2 < B:
                    x2T_copy(s - 2)
                    store_normed(s - 2)
                if 0 <= s - 1 < B:
                    exponentials(s - 1)
                if 0 <= s - 2 < B:
                    second_exp(s - 2)
                if s < B:
                    outT_copy(s)
                if s + 1 < B:
                    pT_copy(s + 1)
                if s == 0:
                    kvT_copy(1)
                    act.wait_ge(b1_t, 1)
                    nc.scalar.copy(b1_sb[:, :], bank[6][:, 0:E * FC]).then_inc(b1_ok, 1)
                if s < EARLY:
                    high_half(s)
            for b in range(B):
                combT_copy(b)
            for b in range(B):
                store_residual(b)

            act.wait_ge(b1_ok, 1)
            act.wait_ge(plan_ok, 1)
            act.wait_ge(rows_out, 16 * B)
            act.wait_ge(meta_in, 16)
            nc.scalar.preload_act_table(ACT.Gelu_apprx_tanh)
            tile = act.alloc_register("act_tile")
            act.reg_mov(tile, 0)

            def token_high(n):
                act.wait_ge(xg_t, n)
                nc.scalar.activation(xhi[:, :, :].rearrange("p c t -> p (c t)"), bank[5][:, 0:D], ACT.Copy,
                                     scale=X_SCALE).then_inc(xhi_ok, 1)

            def expert_tile(e, chunk):
                g = act.snap(tile, min_val=0, max_val=MAXT - 1)
                for q in range(FC // 2):
                    act.wait_ge(h_mm, g * 4 + q + 1)
                    for r in range(2):
                        f = 2 * q + r
                        nc.scalar.activation(hact[:, f, :], bank[q][:, r * P:r * P + P], ACT.Gelu_apprx_tanh,
                                             bias=b1_sb[:, e * FC + f:e * FC + f + 1],
                                             scale=1.0 / (X_SCALE * W_SCALE)).then_inc(act_ok, 1)
                token_high(g + 2)
                if chunk is not None:
                    high_half(chunk)
                act.wait_ge(y_mm, g + 1)
                act.wait_ge(ysb_free, g + 1)
                nc.scalar.activation(ysb[:, :], bank[4][:, 0:D], ACT.Copy,
                                     scale=wcur[:, :].bitcast(F32)).then_inc(y_ok, 1)
                act.reg_add(tile, tile, 1)

            act.sem_inc(y_ok, 1)
            token_high(1)
            tiles_of = [act.value_load(ntile[0:1, e:e + 1], min_val=0, max_val=JT) for e in range(E)]
            for e in range(E):
                tiles_e = tiles_of[e]
                for j in range(PEEL):
                    chunk = 2 * e + EARLY + j if j < 2 and 2 * e + EARLY < NW else None
                    with act.If(tiles_e > j):
                        expert_tile(e, chunk)
                    if chunk is not None:
                        with act.Else():
                            high_half(chunk)
                with act.If(tiles_e > PEEL):
                    with act.Fori(PEEL, JT) as j:
                        with act.If(tiles_e > j):
                            expert_tile(e, None)

        @block.gpsimd
        def _(pool):
            pg = nc.gpsimd
            steps = [0]

            def link(ins):
                steps[0] += 1
                ins.then_inc(pool_step, 1)
                pool.wait_ge(pool_step, steps[0])

            link(pg.memset(ident[:, :], 0.0))
            pg.affine_select(out=ident[:, :], in_=ident[:, :], compare_op=ALU.not_equal, fill=1.0, base=0,
                             pattern=[[-1, P]], channel_multiplier=1).then_inc(ident_ok, 1)
            link(pg.memset(halfneg[:, :], -0.5))

            def deviation(k, b):
                t = slice(HB * b, HB * b + HB)
                return pg.tensor_tensor(rstd[:, k, t], veps[:, k, t], halfneg[:, 0:HB], ALU.pow)

            def normed(k, b):
                link(deviation(k, b))
                for i in range(HB * b, HB * b + HB):
                    ins = pg.tensor_scalar(xn[:, i, :], xs[:, i, :], mneg[:, k, i:i + 1], rstd[:, k, i:i + 1],
                                           ALU.add, ALU.mult)
                    ins.then_inc(xn1_ok if k == 0 else xn2_ok, 1)

            for b in range(B):
                pool.wait_ge(mv1_ok, b + 1)
                normed(0, b)
            link(pg.memset(ones[:, :], 1.0))
            pg.affine_select(out=before[:, :], in_=ones[:, :], compare_op=ALU.is_gt, fill=0.0, base=0,
                             pattern=[[1, P]], channel_multiplier=-1).then_inc(consts, 1)
            pg.memset(zeros[:, :], 0.0).then_inc(consts, 1)
            pg.iota(iota_e[:, :], [[1, E]], base=0, channel_multiplier=0,
                    allow_small_or_imprecise_dtypes=True).then_inc(consts, 1)
            pg.iota(giota[:, :], [[1, MAXT + 2]], base=0, channel_multiplier=0,
                    allow_small_or_imprecise_dtypes=True).then_inc(consts, 1)
            for k in range(KTOP):
                pg.iota(entry[:, :, k, 0:1], [[P, TT], [1, 1]], base=0, channel_multiplier=1).then_inc(consts, 1)
            link(pg.memset(meta[:, :, :], 0))
            pg.iota(meta[:, :, 0:1], [[0, E * JT], [1, 1]], base=N, channel_multiplier=1).then_inc(consts, 1)

            for s in range(STEPS):
                if 0 <= s - 1 < B:
                    pool.wait_ge(mv3_ok, s)
                    pool.wait_ge(p_t, s)
                    normed(2, s - 1)
                if s < B:
                    t = slice(HB * s, HB * s + HB)
                    pool.wait_ge(mv2_ok, s + 1)
                    link(deviation(1, s))
                    pg.tensor_tensor(nmr[:, t], mneg[:, 1, t], rstd[:, 1, t], ALU.mult).then_inc(rstd2_ok, 1)
                if 0 <= s - 2 < B:
                    b = s - 2
                    pool.wait_ge(slot_ok, b + 1)
                    if b == 0:
                        pool.wait_ge(pads_out, 48)
                    for i in range(HB * b, HB * b + HB):
                        for k in range(KTOP):
                            pool.indirect_dma_start(
                                out=table, out_offset=bass.IndirectOffsetOnAxis(slot[:, i, k:k + 1].bitcast(U32), 0),
                                in_=entry[:, i, k, :], in_offset=None).then_inc(entry_out, 16)
            pool.wait_ge(plan_ok, 1)
            pool.wait_ge(meta_in, 16)
            pool.wait_ge(rows_out, 16 * B)
            pool.wait_ge(res_out, 16 * B)
            total = pool.value_load(cendi[0:1, E - 1:E], min_val=16, max_val=MAXT)


            def gather(g, first=False):
                col = pool.value_load(coli[0:1, bass.ds(g, 1)], min_val=0, max_val=E * JT - 1)
                if not first:
                    pool.wait_ge(xg_t, g)
                pg.tensor_copy(gidx[:, :], meta[:, bass.ds(col, 1), 0:1].rearrange("p a b -> p (a b)")
                               ).then_inc(gidx_ok, 1)
                pool.wait_ge(gidx_ok, 1)
                pool.indirect_dma_start(
                    out=xg[:, :], out_offset=None, in_=xn_rows,
                    in_offset=bass.IndirectOffsetOnAxis(gidx[:, :].bitcast(U32), 0)).then_inc(xg_in, 16)
                pool.sem_clear(gidx_ok)

            def add_rows(g, first=False):
                col = pool.value_load(coli[0:1, bass.ds(g, 1)], min_val=0, max_val=E * JT - 1)
                if not first:
                    pool.wait_ge(added, g * 16)
                pg.tensor_copy(wcur[:, :], meta[:, bass.ds(col, 1), 1:2].rearrange("p a b -> p (a b)")
                               ).then_inc(ysb_free, 1)
                pool.wait_ge(y_ok, g + 2)
                pg.tensor_copy(sidx[:, :], meta[:, bass.ds(col, 1), 0:1].rearrange("p a b -> p (a b)")
                               ).then_inc(sidx_ok, 1)
                pool.wait_ge(sidx_ok, 1)
                pool.indirect_dma_start(
                    out=out, out_offset=bass.IndirectOffsetOnAxis(sidx[:, :].bitcast(U32), 0),
                    in_=ysb[:, :], in_offset=None, compute_op=ALU.add).then_inc(added, 16)
                pool.sem_clear(sidx_ok)

            gather(0, first=True)
            gather(1)
            gather(2)
            add_rows(0, first=True)
            with pool.Fori(1, MAXT) as g:
                with pool.If(g + 1 < total):
                    gather(g + 2)
                with pool.If(g < total):
                    add_rows(g)
            pool.wait_ge(added, total * 16)

        @block.vector
        def _(dve):
            v = nc.vector
            steps = [0]

            def link(ins):
                steps[0] += 1
                ins.then_inc(dve_step, 1)
                dve.wait_ge(dve_step, steps[0])

            def mark(ins):
                steps[0] += 1
                ins.then_inc(dve_step, 1)

            v.memset(ctxT[C:C + 1, :], 1.0).then_inc(ones_row, 1)
            mark(v.memset(zer8[:, :], 0.0))

            def tiles(b):
                return range(HB * b, HB * b + HB)

            def aggregate(k, b, eps, ready):
                t = slice(HB * b, HB * b + HB)
                dve.wait_ge(dve_step, steps[0])
                for i in tiles(b):
                    mark(v.bn_aggr(mv[:, k, i, :], st[:, k, i, :]))
                dve.wait_ge(dve_step, steps[0])
                mark(v.tensor_scalar(mneg[:, k, t], mv[:, k, t, 0], -1.0, None, ALU.mult))
                v.tensor_scalar(veps[:, k, t], mv[:, k, t, 1], eps, None, ALU.add).then_inc(ready, 1)

            def input_stats(b):
                dve.wait_ge(x_in[b], 16)
                for i in tiles(b):
                    mark(v.bn_stats(st[:, 0, i, :], xs[:, i, :]))
                aggregate(0, b, LN_EPS, mv1_ok)

            def sim_stats(b):
                for h in range(HB):
                    dve.wait_ge(sim_mm, HB * b + h + 1)
                    mark(v.bn_stats(st[:, 1, HB * b + h, :], bank[4 + h][:, 0:S]))
                aggregate(1, b, SIM_EPS, mv2_ok)

            def affine(b):
                dve.wait_ge(simn_ok, HB * (b + 1))
                link(v.tensor_tensor(sim[:, b % 2, :, :], sim[:, b % 2, :, :],
                                     neggamma[:, :].unsqueeze(1).broadcast_to([P, HB, S]), ALU.mult))
                for h in range(HB):
                    i = HB * b + h
                    v.tensor_tensor_reduce(sim[:, b % 2, h, :], sim[:, b % 2, h, :], negbeta[:, :], 1.0, 3.0e38,
                                           ALU.add, ALU.min, negmax[:, i:i + 1]).then_inc(aff_ok, 1)

            def residual(b):
                t = slice(HB * b, HB * b + HB)
                dve.wait_ge(exp_ok, HB * (b + 1))
                link(v.reciprocal(rsum[:, t], esum[:, t]))
                link(v.tensor_scalar(coef[:, t], rsum[:, t], gates[:, 0:1], None, ALU.mult))
                for h in range(HB):
                    i = HB * b + h
                    mark(v.scalar_tensor_tensor(out=xs[:, i, :], in0=sim[:, b % 2, h, :], scalar=coef[:, i:i + 1],
                                                in1=xs[:, i, :], op0=ALU.mult, op1=ALU.add))
                dve.wait_ge(dve_step, steps[0])
                for i in tiles(b):
                    mark(v.bn_stats(st[:, 2, i, :], xs[:, i, :]))
                aggregate(2, b, LN_EPS, mv3_ok)

            def top_two(b):
                t = slice(HB * b, HB * b + HB)
                dve.wait_ge(lg_mm, b + 1)
                link(v.tensor_tensor(lg[:, t, :], bank[6][:, 0:HB * E].rearrange("p (h e) -> p h e", h=HB),
                                     gb[:, :].unsqueeze(1).broadcast_to([P, HB, E]), ALU.add))
                for i in tiles(b):
                    mark(v.max(mx[:, i, :], lg[:, i, :]))
                dve.wait_ge(dve_step, steps[0])
                v.tensor_tensor(dif[:, t], mx[:, t, 1], mx[:, t, 0], ALU.subtract).then_inc(dif_ok, 1)
                for i in tiles(b):
                    mark(v.max_index(ix[:, i, :], mx[:, i, :], lg[:, i, :]))
                dve.wait_ge(dve_step, steps[0])
                link(v.tensor_copy(ixf[:, t, :], ix[:, t, 0:KTOP]))
                link(v.tensor_tensor(mask[:, t, :, :].rearrange("p h k e -> p (h k) e"),
                                     iota_e[:, :].unsqueeze(1).broadcast_to([P, HB * KTOP, E]),
                                     ixf[:, t, :].rearrange("p h k -> p (h k)").unsqueeze(2).broadcast_to(
                                         [P, HB * KTOP, E]), ALU.is_equal))
                v.tensor_tensor(mcount[:, t, :], mask[:, t, 0, :], mask[:, t, 1, :], ALU.add).then_inc(mask_ok, 1)

            def weights(b):
                t = slice(HB * b, HB * b + HB)
                dve.wait_ge(e2_ok, b + 1)
                link(v.tensor_scalar(den[:, t], e2[:, t], 1.0, None, ALU.add))
                link(v.reciprocal(wk2[:, t, 0], den[:, t]))
                link(v.tensor_tensor(wk2[:, t, 1], e2[:, t], wk2[:, t, 0], ALU.mult))
                mark(v.tensor_scalar(entry[:, t, :, 1].bitcast(F32), wk2[:, t, :], gslot[:, 0:1], None, ALU.mult))

            def token_weights(b):
                t = slice(HB * b, HB * b + HB)
                link(v.tensor_tensor(wmask[:, t, :, :].rearrange("p h k e -> p (h k) e"),
                                     mask[:, t, :, :].rearrange("p h k e -> p (h k) e"),
                                     wk2[:, t, :].rearrange("p h k -> p (h k)").unsqueeze(2).broadcast_to(
                                         [P, HB * KTOP, E]), ALU.mult))
                v.tensor_tensor(comb[:, t, :], wmask[:, t, 0, :], wmask[:, t, 1, :], ALU.add).then_inc(comb_ok, 1)

            def slots(b):
                t = slice(HB * b, HB * b + HB)
                dve.wait_ge(rank_mm, b + 1)
                link(v.tensor_tensor(rmask[:, t, :, :],
                                     bank[7][:, 0:HB * E].rearrange("p (h e) -> p h e", h=HB).unsqueeze(2).broadcast_to(
                                         [P, HB, KTOP, E]),
                                     mask[:, t, :, :], ALU.mult))
                with nc.allow_low_precision(reason="whole numbers below 1024"):
                    link(v.tensor_reduce(ranki[:, t, :], rmask[:, t, :, :], mybir.AxisListType.X, ALU.add))
                link(v.tensor_scalar(rlow[:, t, :], ranki[:, t, :], P - 1, 6, ALU.bitwise_and, ALU.logical_shift_left))
                link(v.scalar_tensor_tensor(out=rrow[:, t, :], in0=ranki[:, t, :], scalar=7, in1=rlow[:, t, :],
                                            op0=ALU.logical_shift_right, op1=ALU.bitwise_or))
                v.scalar_tensor_tensor(out=slot[:, t, :], in0=ix[:, t, 0:KTOP].bitcast(I32), scalar=3,
                                       in1=rrow[:, t, :], op0=ALU.logical_shift_left,
                                       op1=ALU.bitwise_or).then_inc(slot_ok, 1)

            def bias_out(b):
                t = slice(HB * b, HB * b + HB)
                dve.wait_ge(b2_mm, b + 1)
                v.scalar_tensor_tensor(out=xs[:, t, :].rearrange("p h d -> p (h d)"), in0=bank[1][:, :],
                                       scalar=gates[:, 1:2], in1=xs[:, t, :].rearrange("p h d -> p (h d)"),
                                       op0=ALU.mult, op1=ALU.add).then_inc(res_ok, 1)

            def low_part(n, q):
                if q == 0:
                    dve.wait_ge(w_in[n % STG], 16 * (n // STG + 1))
                r = slice(q * CH // 4, (q + 1) * CH // 4)
                dve.wait_ge(hi_ok, 4 * n + q + 1)
                v.scalar_tensor_tensor(out=wlo[:, n // 2, n % 2, r], in0=w_stage(n)[:, r], scalar=W_SCALE,
                                       in1=whi[:, n // 2, n % 2, r], op0=ALU.mult,
                                       op1=ALU.subtract).then_inc(lo_ok, 1)

            for b in range(B):
                input_stats(b)
            dve.wait_ge(small_in, 16 * NSMALL)
            mark(v.tensor_scalar(neggamma[:, :], neggamma[:, :], -1.0, None, ALU.mult))
            mark(v.tensor_scalar(negbeta[:, :], negbeta[:, :], -1.0, None, ALU.mult))
            dve.wait_ge(tanh_ok, 1)
            mark(v.tensor_scalar(gslot[:, :], gates[:, 1:2], 1.0 / (H_SCALE * W_SCALE), None, ALU.mult))
            for s in range(STEPS):
                if 0 <= s - 1 < B:
                    affine(s - 1)
                if 0 <= s - 2 < B:
                    top_two(s - 2)
                if 0 <= s - 1 < B:
                    residual(s - 1)
                if 0 <= s - 2 < B:
                    weights(s - 2)
                    slots(s - 2)
                if s < B:
                    sim_stats(s)
                if s >= STEPS - EARLY + 1:
                    for q in range(4):
                        low_part(s - (STEPS - EARLY + 1), q)
            for b in range(B):
                token_weights(b)

            dve.wait_ge(cnt_mm, 1)
            link(v.tensor_copy(cnti[:, :], bank[7][0:1, 64:64 + E]))
            link(v.tensor_scalar(cntr[:, :], cnti[:, :], P - 1, None, ALU.add))
            link(v.tensor_scalar(ntile[:, :], cntr[:, :], 7, None, ALU.logical_shift_right))
            link(v.tensor_copy(ntf[:, :], ntile[:, :]))
            link(v.tensor_tensor_scan(cend[:, :], ntf[:, :], zer8[:, :], 0.0, ALU.add, ALU.add))
            mark(v.tensor_copy(cendi[:, :], cend[:, :]))
            link(v.tensor_tensor(past[:, :, :], cend[:, :].unsqueeze(1).broadcast_to([1, MAXT + 2, E]),
                                 giota[:, :].unsqueeze(2).broadcast_to([1, MAXT + 2, E]), ALU.is_le))
            mark(v.tensor_tensor(pastn[:, :, :], past[:, :, :], ntf[:, :].unsqueeze(1).broadcast_to([1, MAXT + 2, E]),
                                 ALU.mult))
            link(v.tensor_reduce(eg[:, :], past[:, :, :], mybir.AxisListType.X, ALU.add))
            mark(v.tensor_scalar(egi[:, :], eg[:, :], float(FC), None, ALU.mult))
            link(v.tensor_reduce(sg[:, :], pastn[:, :, :], mybir.AxisListType.X, ALU.add))
            link(v.tensor_tensor(col1[:, :], giota[:, :], sg[:, :], ALU.subtract))
            link(v.scalar_tensor_tensor(out=col2[:, :], in0=eg[:, :], scalar=float(JT), in1=col1[:, :],
                                        op0=ALU.mult, op1=ALU.add))
            v.tensor_scalar(coli[:, :], col2[:, :], float(E * JT - 1), None, ALU.min).then_inc(plan_ok, 1)

            def token_low(n):
                dve.wait_ge(xhi_ok, n)
                v.scalar_tensor_tensor(out=xlo[:, :, :].rearrange("p c t -> p (c t)"), in0=bank[5][:, 0:D],
                                       scalar=X_SCALE, in1=xhi[:, :, :].rearrange("p c t -> p (c t)"),
                                       op0=ALU.mult, op1=ALU.subtract).then_inc(xlo_ok, 1)

            def expert_tile(chunk):
                g = dve.snap(tile, min_val=0, max_val=MAXT - 1)
                for q in range(FC // 2):
                    f = slice(2 * q, 2 * q + 2)
                    dve.wait_ge(act_ok, g * FC + 2 * q + 2)
                    v.tensor_scalar(hhi[:, f, :], hact[:, f, :], H_SCALE, None, ALU.mult).then_inc(hhi_ok, 1)
                    dve.wait_ge(hhi_ok, g * 4 + q + 1)
                    v.scalar_tensor_tensor(out=hlo[:, f, :], in0=hact[:, f, :], scalar=H_SCALE,
                                           in1=hhi[:, f, :], op0=ALU.mult, op1=ALU.subtract).then_inc(hsplit_ok, 1)
                token_low(g + 2)
                if chunk is not None:
                    for q in range(4):
                        low_part(chunk, q)
                dve.reg_add(tile, tile, 1)

            for b in range(B):
                bias_out(b)
            for q in range(4):
                low_part(EARLY - 1, q)
            dve.wait_ge(plan_ok, 1)
            tile = dve.alloc_register("dve_tile")
            dve.reg_mov(tile, 0)
            token_low(1)
            tiles_of = [dve.value_load(ntile[0:1, e:e + 1], min_val=0, max_val=JT) for e in range(E)]
            for e in range(E):
                tiles_e = tiles_of[e]
                for j in range(PEEL):
                    chunk = 2 * e + EARLY + j if j < 2 and 2 * e + EARLY < NW else None
                    with dve.If(tiles_e > j):
                        expert_tile(chunk)
                    if chunk is not None:
                        with dve.Else():
                            for q in range(4):
                                low_part(chunk, q)
                with dve.If(tiles_e > PEEL):
                    with dve.Fori(PEEL, JT) as j:
                        with dve.If(tiles_e > j):
                            expert_tile(None)

        @block.tensor
        def _(pe):
            pe.wait_ge(ident_ok, 1)
            pe.wait_ge(ctx_in, 48)
            pe.transpose(bank[7][0:C, 0:C], wk_sb[:, :], ident[0:C, 0:C]).then_inc(wk_t, 1)
            for i in range(TT):
                t = pe.transpose(bank[i // 4][0:C, i % 4 * P:i % 4 * P + P], ctx_sb[:, i, :], ident[:, :])
                if i % 4 == 3:
                    t.then_inc(ctx_t, 1)
            pe.wait_ge(wkT_ok, 1)
            pe.wait_ge(ones_row, 1)

            def keys(i):
                pe.wait_ge(ctxT_ok, i + 1)
                pe.matmul(bank[2 + i][0:C, :], wkT[:, :], ctxT[:, i * 512:i * 512 + 512],
                          start=True, stop=True).then_inc(kvT_mm, 1)

            def values():
                pe.wait_ge(ctxT_ok, 2)
                for i in range(TT):
                    m = pe.matmul(bank[4][:, i * C:i * C + C], ctxT[:, i * P:i * P + P], wkT[:, :],
                                  start=True, stop=True)
                m.then_inc(kv_mm, 1)

            def transpose_p(b):
                pe.wait_ge(xn1_ok, HB * (b + 1))
                if b == 0:
                    pe.wait_ge(ctxT_ok, 1)
                else:
                    pe.wait_ge(pT_ok, b)
                for h in range(HB):
                    for c in range(DC):
                        t = pe.transpose(bank[0][:, c * S + h * P:c * S + h * P + P],
                                         xn[:, HB * b + h, c * P:c * P + P], ident[:, :])
                t.then_inc(p_t, 1)

            def attend(b):
                pe.wait_ge(pT_ok, b + 1)
                if b == 0:
                    pe.wait_ge(kv_ok, 1)
                    pe.wait_ge(kvT_ok, 1)
                else:
                    pe.wait_ge(outT_ok, b)
                for c in range(DC):
                    m = pe.matmul(bank[2][0:C, 0:S], kv[:, HB * b + c, :], pT[:, c, :],
                                  start=(c == 0), stop=(c == DC - 1))
                m.then_inc(out_mm, 1)

            def similarities(b):
                pe.wait_ge(outT_ok, b + 1)
                pe.wait_ge(kvT_ok, 1 + b // 2)
                if b >= 1:
                    pe.wait_ge(simn_ok, HB * b)
                for h in range(HB):
                    pe.matmul(bank[4 + h][:, 0:S], outT[:, h * P:h * P + P], kvT[:, b * S:b * S + S],
                              start=True, stop=True).then_inc(sim_mm, 1)

            def logits(b):
                pe.wait_ge(xn2_ok, HB * (b + 1))
                if b == 0:
                    pe.wait_ge(kvT_ok, 2)
                    pe.wait_ge(gate_in, 48)
                else:
                    pe.wait_ge(x2T_ok, b)
                for h in range(HB):
                    for c in range(DC):
                        t = pe.transpose(bank[3][:, c * S + h * P:c * S + h * P + P],
                                         xn[:, HB * b + h, c * P:c * P + P], ident[:, :])
                t.then_inc(x2_t, 1)
                pe.wait_ge(x2T_ok, b + 1)
                if b == 0:
                    pe.wait_ge(b1_ok, 1)
                else:
                    pe.wait_ge(mask_ok, b)
                for h in range(HB):
                    for c in range(DC):
                        m = pe.matmul(bank[6][:, h * E:h * E + E], x2T[:, c, h * P:h * P + P], gw[:, c, :],
                                      start=(c == 0), stop=(c == DC - 1))
                m.then_inc(lg_mm, 1)

            def ranks(b):
                pe.wait_ge(mask_ok, b + 1)
                if b >= 1:
                    pe.wait_ge(slot_ok, b)
                else:
                    pe.wait_ge(consts, NCONST)
                for h in range(HB):
                    i = HB * b + h
                    o = bank[7][:, h * E:h * E + E]
                    m = pe.matmul(o, before[:, :], mcount[:, i, :], start=True, stop=(i == 0))
                    for k in range(i):
                        m = pe.matmul(o, ones[:, :], mcount[:, k, :], start=False, stop=(k == i - 1))
                m.then_inc(rank_mm, 1)

            def bias_rows(b):
                pe.wait_ge(comb_ok, b + 1)
                pe.wait_ge(ctxT_ok, 2)
                if b >= 1:
                    pe.wait_ge(res_ok, b)
                for h in range(HB):
                    t = pe.transpose(bank[1][0:E, h * P:h * P + P], comb[:, HB * b + h, :], ident[:, :])
                t.then_inc(comb_t, 1)
                pe.wait_ge(combT_ok, b + 1)
                for h in range(HB):
                    m = pe.matmul(bank[1][:, h * D:h * D + D], combT[:, h * P:h * P + P], b2_sb[:, :],
                                  start=True, stop=True)
                m.then_inc(b2_mm, 1)

            keys(0)
            values()
            transpose_p(0)
            for s in range(STEPS):
                if 0 <= s - 2 < B:
                    logits(s - 2)
                if s < B:
                    attend(s)
                if s == 0:
                    keys(1)
                    pe.wait_ge(small_in, 16 * NSMALL)
                    pe.transpose(bank[6][:, 0:E * FC], b1_rows[:, :], ident[0:E * FC, 0:E * FC]).then_inc(b1_t, 1)
                if s < B:
                    similarities(s)
                if 0 <= s - 2 < B:
                    ranks(s - 2)
                if s + 1 < B:
                    transpose_p(s + 1)
            pe.wait_ge(slot_ok, B)
            for k in range(TT):
                m = pe.matmul(bank[7][:, 64:64 + E], ones[:, :], mcount[:, k, :], start=(k == 0), stop=(k == TT - 1))
            m.then_inc(cnt_mm, 1)
            for b in range(B):
                bias_rows(b)

            pe.wait_ge(plan_ok, 1)
            pe.wait_ge(res_ok, B)
            tile = pe.alloc_register("pe_tile")
            pe.reg_mov(tile, 0)

            def transpose_tokens(n):
                pe.wait_ge(xg_in, n * 16)
                for c in range(DC):
                    t = pe.transpose(bank[5][:, c * P:c * P + P], xg[:, c * P:c * P + P], ident[:, :])
                t.then_inc(xg_t, 1)

            def expert_tile(e):
                g = pe.snap(tile, min_val=0, max_val=MAXT - 1)
                pe.wait_ge(xlo_ok, g + 1)
                for q in range(FC // 2):
                    for r in range(2):
                        f = 2 * q + r
                        k = 0
                        for c in range(DC):
                            w = slice(c * F + f * P, c * F + f * P + P)
                            for wt, xt in ((whi, xhi), (whi, xlo), (wlo, xhi)):
                                m = pe.matmul(bank[q][:, r * P:r * P + P], wt[:, e, 0, w], xt[:, c, :],
                                              start=(k == 0), stop=(k == 3 * DC - 1))
                                k += 1
                    m.then_inc(h_mm, 1)
                transpose_tokens(g + 2)
                pe.wait_ge(hi_ok, 8 * e + 8)
                pe.wait_ge(lo_ok, 8 * e + 8)
                pe.wait_ge(y_ok, g + 1)
                for f in range(FC):
                    if f % 2 == 0:
                        pe.wait_ge(hsplit_ok, g * 4 + f // 2 + 1)
                    for ht, wt in ((hhi, whi), (hhi, wlo), (hlo, whi)):
                        m = pe.matmul(bank[4][:, 0:D], ht[:, f, :], wt[:, e, 1, f * D:f * D + D],
                                      start=(f == 0 and ht is hhi and wt is whi),
                                      stop=(f == FC - 1 and ht is hlo))
                m.then_inc(y_mm, 1)
                pe.reg_add(tile, tile, 1)

            transpose_tokens(1)
            tiles_of = [pe.value_load(ntile[0:1, e:e + 1], min_val=0, max_val=JT) for e in range(E)]
            for e in range(E):
                tiles_e = tiles_of[e]
                pe.wait_ge(hi_ok, 8 * e + 4)
                pe.wait_ge(lo_ok, 8 * e + 4)
                for j in range(PEEL):
                    with pe.If(tiles_e > j):
                        expert_tile(e)
                with pe.If(tiles_e > PEEL):
                    with pe.Fori(PEEL, JT) as j:
                        with pe.If(tiles_e > j):
                            expert_tile(e)


_INS = ['x', 'ctx_512', 'g_xattn', 'g_ffn', 'L0_xattn_W_k', 'L0_xattn_b_k', 'L0_xattn_ln_gamma', 'L0_xattn_ln_beta',
        'L0_ffn_gate_w', 'L0_ffn_gate_b', 'L0_ffn_w1', 'L0_ffn_b1', 'L0_ffn_w2', 'L0_ffn_b2']


def kernel(**inputs):
    import numpy as _np
    import concourse.bacc as _bacc
    from concourse import mybir as _mybir
    from concourse.bass_utils import run_bass_kernel_spmd as _run

    nc = _bacc.Bacc("TRN2", target_bir_lowering=False, num_devices=1)
    arrays, args = {}, []
    for name in _INS:
        a = _np.ascontiguousarray(inputs[name])
        arrays[f"in_{name}"] = a
        args.append(nc.dram_tensor(f"in_{name}", a.shape, _mybir.dt.from_np(a.dtype), kind="ExternalInput").ap())
    B, S, D = inputs['x'].shape
    out = nc.dram_tensor("out_rows", (B * S + 128, D), _mybir.dt.float32, kind="ExternalOutput").ap()
    gated_block(nc, *args, out)
    r = _run(nc, [arrays], core_ids=[0])
    return r.results[0]["out_rows"][:B * S].reshape(B, S, D)
```

```python
from contextlib import ExitStack

import concourse.bass as bass
from concourse import mybir

ALU = mybir.AluOpType
ACT = mybir.ActivationFunctionType
F32 = mybir.dt.float32
F16 = mybir.dt.float16
BF16 = mybir.dt.bfloat16
I32 = mybir.dt.int32
U32 = mybir.dt.uint32
P = 128

X_SCALE = 2.0 ** 10
W_SCALE = 2.0 ** 10
H_SCALE = 2.0 ** 6
LN_EPS = 1e-5
SIM_EPS = 1e-6


def gated_block(nc, x, ctx_kv, g_xattn, g_ffn, w_k, b_k, ln_gamma, ln_beta,
                gate_w, gate_b, w1, b1, w2, b2, out):
    B, S, D = x.shape
    C = ctx_kv.shape[2]
    E, _, F = w1.shape
    N = B * S
    TT = N // P
    HB = S // P
    DC = D // P
    FC = F // P
    KTOP = 2
    JT = N // P
    MAXT = (KTOP * N + E * (P - 1)) // P
    PAD = P
    STG = 3
    CH = DC * F
    assert DC * F == FC * D and S == D and HB == 2 and DC == 2 and FC == 8 and E == 8

    xn_rows = nc.dram_tensor("xn_rows", (N + PAD, D), F32).ap()

    es = ExitStack()
    with es:
        def sb(name, shape, dt):
            return es.enter_context(nc.sbuf_tensor(name, shape, dt))

        def sem(name):
            return es.enter_context(nc.semaphore(name))

        bank = [es.enter_context(nc.psum_tensor(f"bank{i}", [P, 512], F32)) for i in range(8)]

        whi = sb("whi", [P, E, 2, CH], F16)
        wlo = sb("wlo", [P, E, 2, CH], F16)
        stage = sb("stage", [P, STG, CH], F32)
        xs = sb("xs", [P, TT, D], F32)
        xn = sb("xn", [P, TT, D], F32)
        ctx_sb = sb("ctx_sb", [P, TT, C], F32)
        shared = sb("shared", [P, N], F32)
        ctxT = shared[0:C + 1, :]
        atrow = shared[:, 0:N // 2].rearrange("p (t r) -> p t r", t=HB * KTOP)
        atcol = shared[:, N // 2:N].rearrange("p (t v c) -> p t v c", t=HB * KTOP, v=2)
        wk_sb = sb("wk_sb", [C, C], F32)
        wkT = sb("wkT", [C + 1, C], F32)
        kvT = sb("kvT", [C, N], F32)
        kv = sb("kv", [P, TT, C], F32)
        pT = sb("pT", [P, DC, S], F32)
        outT = sb("outT", [C, S], F32)
        sim = sb("sim", [P, 2, HB, S], F32)
        negbeta = sb("negbeta", [P, S], F32)
        neggamma = sb("neggamma", [P, S], F32)
        x2T = sb("x2T", [P, HB, DC, P], F32)
        gw = sb("gw", [P, DC, E], F32)
        gb = sb("gb", [P, E], F32)
        b2_sb = sb("b2_sb", [E, D], F32)
        b1_rows = sb("b1_rows", [E * FC, P], F32)
        b1_sb = sb("b1_sb", [P, E * FC], F32)
        gates = sb("gates", [P, 2], F32)
        gslot = sb("gslot", [P, 1], F32)
        ident = sb("ident", [P, P], F32)
        before = sb("before", [P, P], BF16)
        ones = sb("ones", [P, P], BF16)
        zeros = sb("zeros", [P, D], F32)
        halfneg = sb("halfneg", [P, HB], F32)
        one = sb("one", [P, HB], F32)
        negone = sb("negone", [P, HB], F32)
        st = sb("st", [P, 3, TT, 6], F32)
        mv = sb("mv", [P, 3, TT, 2], F32)
        veps = sb("veps", [P, 3, TT], F32)
        rstd = sb("rstd", [P, 3, TT], F32)
        mneg = sb("mneg", [P, 3, TT], F32)
        nmr = sb("nmr", [P, TT], F32)
        negmax = sb("negmax", [P, TT], F32)
        esum = sb("esum", [P, TT], F32)
        rsum = sb("rsum", [P, TT], F32)
        coef = sb("coef", [P, TT], F32)
        lg = sb("lg", [P, TT, E], F32)
        mx = sb("mx", [P, TT, 8], F32)
        ix = sb("ix", [P, TT, 8], U32)
        ixf = sb("ixf", [P, TT, KTOP], F32)
        iota_e = sb("iota_e", [P, E], F32)
        dif = sb("dif", [P, TT], F32)
        e2 = sb("e2", [P, TT], F32)
        den = sb("den", [P, TT], F32)
        wk2 = sb("wk2", [P, TT, KTOP], F32)
        mask = sb("mask", [P, TT, KTOP, E], F32)
        mcount = sb("mcount", [P, TT, E], BF16)
        wmask = sb("wmask", [P, TT, KTOP, E], F32)
        comb = sb("comb", [P, TT, E], F32)
        combT = sb("combT", [E, HB * P], F32)
        rmask = sb("rmask", [P, TT, KTOP, E], F32)
        ranki = sb("ranki", [P, TT, KTOP], I32)
        rhigh = sb("rhigh", [P, TT, KTOP], I32)
        rc = sb("rc", [P, TT, KTOP, 2], I32)
        rcf = sb("rcf", [P, TT, KTOP, 2], F32)
        vals = sb("vals", [P, TT, KTOP, 2], F32)
        colhot = sb("colhot", [P, HB * KTOP, E * JT], F32)
        iota_r = sb("iota_r", [P, P], F32)
        iota_p = sb("iota_p", [P, 1], F32)
        padid = sb("padid", [P, E * JT], F32)
        ids = sb("ids", [P, E * JT], I32)
        wts = sb("wts", [P, E * JT], F32)
        cntr = sb("cntr", [1, E], I32)
        ntile = sb("ntile", [1, E], I32)
        ngap = sb("ngap", [1, E], F32)
        ntf = sb("ntf", [1, E], F32)
        pow16 = sb("pow16", [1, E], F32)
        npow = sb("npow", [1, E], F32)
        packed = sb("packed", [1, 2], I32)
        zer8 = sb("zer8", [1, E], F32)
        cend = sb("cend", [1, E], F32)
        cendi = sb("cendi", [1, E], I32)
        giota = sb("giota", [1, MAXT + 3], F32)
        past = sb("past", [1, MAXT + 3, E], F32)
        pastn = sb("pastn", [1, MAXT + 3, E], F32)
        sg = sb("sg", [1, MAXT + 3], F32)
        col1 = sb("col1", [1, MAXT + 3], F32)
        coli = sb("coli", [1, MAXT + 3], I32)
        gidx = sb("gidx", [P, 1], I32)
        sidx = sb("sidx", [P, 1], I32)
        wcur = sb("wcur", [P, 2], F32)
        xhi = sb("xhi", [P, DC, P], F16)
        xlo = sb("xlo", [P, DC, P], F16)
        hact = xn[:, 0:4, :].rearrange("p a b -> p (a b)").rearrange("p (f t) -> p f t", f=FC)
        hhi = xn[:, 4:6, :].bitcast(F16).rearrange("p a b -> p (a b)").rearrange("p (f t) -> p f t", f=FC)
        hlo = xn[:, 6:8, :].bitcast(F16).rearrange("p a b -> p (a b)").rearrange("p (f t) -> p f t", f=FC)
        xg = ctx_sb[:, 0:4, :].rearrange("p a b -> p (a b)")
        ysb = sim[:, 0, :, :]

        x_in = [sem(f"x_in{b}") for b in range(B)]
        ctx_in = sem("ctx_in")
        wk_in = sem("wk_in")
        ones_ok = sem("ones_ok")
        small_in = sem("small_in")
        pads_out = sem("pads_out")
        w_in = [[sem(f"w_in{i}_{q}") for q in range(4)] for i in range(STG)]
        consts = sem("consts")
        wk_t = sem("wk_t")
        wkT_ok = sem("wkT_ok")
        b1_t = sem("b1_t")
        b1_ok = sem("b1_ok")
        ctx_t = sem("ctx_t")
        ctxT_ok = sem("ctxT_ok")
        kv_mm = sem("kv_mm")
        kv_ok = sem("kv_ok")
        kvT_mm = sem("kvT_mm")
        kvT_ok = sem("kvT_ok")
        gate_in = sem("gate_in")
        ident_ok = sem("ident_ok")
        ones_row = sem("ones_row")
        tanh_ok = sem("tanh_ok")
        dve_step = sem("dve_step")
        pool_step = sem("pool_step")
        mv1_ok = sem("mv1_ok")
        xn1_ok = sem("xn1_ok")
        p_t = sem("p_t")
        pT_ok = sem("pT_ok")
        out_mm = sem("out_mm")
        outT_ok = sem("outT_ok")
        sim_mm = sem("sim_mm")
        mv2_ok = sem("mv2_ok")
        rstd2_ok = sem("rstd2_ok")
        simn_ok = sem("simn_ok")
        aff_ok = sem("aff_ok")
        exp_ok = sem("exp_ok")
        mv3_ok = sem("mv3_ok")
        xn2_ok = sem("xn2_ok")
        rows_out = sem("rows_out")
        x2_t = sem("x2_t")
        x2T_ok = sem("x2T_ok")
        lg_mm = sem("lg_mm")
        gslot_ok = sem("gslot_ok")
        vals_ok = sem("vals_ok")
        dif_ok = sem("dif_ok")
        e2_ok = sem("e2_ok")
        mask_ok = sem("mask_ok")
        rank_mm = sem("rank_mm")
        slot_ok = sem("slot_ok")
        atrow_ok = sem("atrow_ok")
        atcol_ok = sem("atcol_ok")
        place_mm = sem("place_mm")
        comb_ok = sem("comb_ok")
        comb_t = sem("comb_t")
        combT_ok = sem("combT_ok")
        b2_mm = sem("b2_mm")
        res_ok = sem("res_ok")
        res_out = sem("res_out")
        hi_ok = sem("hi_ok")
        lo_ok = sem("lo_ok")
        tiles_ok = sem("tiles_ok")
        plan_ok = sem("plan_ok")
        meta_ok = sem("meta_ok")
        gidx_ok = sem("gidx_ok")
        xg_in = sem("xg_in")
        xg_t = sem("xg_t")
        xhi_ok = sem("xhi_ok")
        xlo_ok = sem("xlo_ok")
        h_mm = sem("h_mm")
        act_ok = sem("act_ok")
        hhi_ok = sem("hhi_ok")
        hsplit_ok = sem("hsplit_ok")
        y_mm = sem("y_mm")
        y_ok = sem("y_ok")
        sidx_ok = sem("sidx_ok")
        added = sem("added")
        ysb_free = sem("ysb_free")

        NSMALL = 5
        KEYS = [(0, S, 5), (S, S, 3), (2 * S, 2 * S, 1)]
        NCONST = 7
        STEPS = B + 2
        NW = 2 * E
        HIGH_AT = [[(0, 2), (0, 3)], [], [(1, 3), (2, 0), (2, 1)], [(2, 2), (2, 3)], [], []]
        LOW_AT = [[(0, 0), (0, 1)], [], [(0, 2), (0, 3), (1, 0)], [], [], [(1, 1), (1, 2)]]
        PEEL = 3
        EARLY = 3

        def w_dram(n):
            e, which = divmod(n, 2)
            src = w2 if which else w1
            return src[e].rearrange("(c p) n -> p c n", p=P)

        def w_stage(n):
            return stage[:, n % STG, :]

        def splits(e, j):
            n = 2 * e + EARLY + j
            return [(n, q) for q in range(4)] if j < 2 and n < NW else []

        block = es.enter_context(nc.Block())

        def tile_counts(eng):
            return [eng.value_load(packed[0:1, i:i + 1], min_val=0, max_val=(JT << 12) + (JT << 8) + (JT << 4) + JT)
                    for i in range(2)]

        def tiles_of(eng, counts, e):
            return eng.snap((counts[e // 4] >> (4 * (e % 4))) & 15, min_val=0, max_val=JT)

        @block.sync
        def _(sp):
            sp.dma_start(xs[:, 0:HB, :], x[0].rearrange("(h p) d -> p h d", p=P)).then_inc(x_in[0], 16)
            sp.dma_start(wkT[C:C + 1, :], b_k.unsqueeze(0)).then_inc(wk_in, 16)
            for b in range(1, B):
                sp.dma_start(xs[:, HB * b:HB * b + HB, :],
                             x[b].rearrange("(h p) d -> p h d", p=P)).then_inc(x_in[b], 16)
            sp.dma_start(gates[:, 0:1], g_xattn.partition_broadcast(P)).then_inc(small_in, 16)
            sp.dma_start(gates[:, 1:2], g_ffn.partition_broadcast(P)).then_inc(small_in, 16)
            sp.dma_start(neggamma[:, :], ln_gamma.partition_broadcast(P)).then_inc(small_in, 16)
            sp.dma_start(negbeta[:, :], ln_beta.partition_broadcast(P)).then_inc(small_in, 16)
            sp.dma_start(b1_rows[:, :], b1.rearrange("e (c p) -> (e c) p", p=P)).then_inc(small_in, 16)
            sp.dma_start(gw[:, :, :], gate_w.rearrange("(c p) e -> p c e", p=P)).then_inc(gate_in, 16)
            sp.dma_start(gb[:, :], gate_b.partition_broadcast(P)).then_inc(gate_in, 16)
            sp.dma_start(b2_sb[:, :], b2).then_inc(gate_in, 16)

            def load_weights(n):
                if n == EARLY + 2:
                    sp.wait_ge(xg_in, 32)
                for q in range(4):
                    if n >= STG:
                        sp.wait_ge(hi_ok, 4 * (n - STG) + q + 1)
                        sp.wait_ge(lo_ok, 4 * (n - STG) + q + 1)
                    r = slice(q * CH // 4, (q + 1) * CH // 4)
                    if n % 2 == 0:
                        c, half = divmod(q, 2)
                        src = w_dram(n)[:, c, half * F // 2:(half + 1) * F // 2]
                        dst = w_stage(n)[:, r]
                    else:
                        src = w_dram(n)[:, q * FC // 4:(q + 1) * FC // 4, :]
                        dst = w_stage(n)[:, r].rearrange("p (c n) -> p c n", c=FC // 4)
                    sp.dma_start(dst, src).then_inc(w_in[n % STG][q], 16)

            for n in range(STG):
                load_weights(n)
            sp.wait_ge(consts, NCONST)
            sp.dma_start(xn_rows[N:N + PAD, :], zeros[:, :]).then_inc(pads_out, 16)
            sp.dma_start(out[N:N + PAD, :], zeros[:, :]).then_inc(pads_out, 16)
            for n in range(STG, NW):
                load_weights(n)

        @block.scalar
        def _(act):
            act.dma_start(ctx_sb[:, :, :], ctx_kv.rearrange("b (h p) c -> p (b h) c", p=P)).then_inc(ctx_in, 16)
            act.dma_start(wk_sb[:, :], w_k).then_inc(wk_in, 16)
            nc.scalar.preload_act_table(ACT.Exp)

            def ctxT_copy(i):
                act.wait_ge(ctx_t, i + 1)
                nc.scalar.copy(ctxT[0:C, i * 512:i * 512 + 512], bank[1 + 5 * i][0:C, :]).then_inc(ctxT_ok, 1)

            def kvT_copy(i):
                act.wait_ge(kvT_mm, i + 1)
                at, n, o = KEYS[i]
                nc.scalar.copy(kvT[:, at:at + n], bank[o][0:C, 0:n]).then_inc(kvT_ok, 1)

            def x2T_copy(b):
                if b >= 1:
                    act.wait_ge(lg_mm, b)
                for h in range(HB):
                    act.wait_ge(x2_t, HB * b + h + 1)
                    nc.scalar.copy(x2T[:, h, :, :].rearrange("p c s -> p (c s)"),
                                   bank[3 - 2 * h][:, 0:D]).then_inc(x2T_ok, 1)

            def normalise(b):
                act.wait_ge(rstd2_ok, b + 1)
                for h in range(HB):
                    i = HB * b + h
                    nc.scalar.activation(sim[:, b % 2, h, :], bank[4 + h][:, 0:S], ACT.Identity,
                                         bias=nmr[:, i:i + 1], scale=rstd[:, 1, i:i + 1]).then_inc(simn_ok, 1)

            def outT_copy(b):
                act.wait_ge(out_mm, b + 1)
                if b >= 1:
                    act.wait_ge(sim_mm, b)
                nc.scalar.mul(outT[:, :], bank[2][0:C, 0:S], float(D) ** -0.5).then_inc(outT_ok, 1)

            def exponentials(b):
                for h in range(HB):
                    i = HB * b + h
                    act.wait_ge(aff_ok, i + 1)
                    nc.scalar.activation(sim[:, b % 2, h, :], sim[:, b % 2, h, :], ACT.Exp,
                                         bias=negmax[:, i:i + 1], scale=-1.0,
                                         accum_out=esum[:, i:i + 1]).then_inc(exp_ok, 1)

            def second_exp(b):
                t = slice(HB * b, HB * b + HB)
                act.wait_ge(dif_ok, b + 1)
                nc.scalar.activation(e2[:, t], dif[:, t], ACT.Exp).then_inc(e2_ok, 1)

            def combT_copy(b):
                act.wait_ge(comb_t, b + 1)
                if b >= 1:
                    act.wait_ge(b2_mm, b)
                nc.scalar.copy(combT[:, :], bank[b % 2 * 2][0:E, 0:HB * P]).then_inc(combT_ok, 1)

            def pT_copy(b):
                act.wait_ge(p_t, b + 1)
                if b >= 1:
                    act.wait_ge(out_mm, b)
                nc.scalar.copy(pT[:, :, :].rearrange("p c s -> p (c s)"), bank[0][:, :]).then_inc(pT_ok, 1)

            def high_part(n, q):
                act.wait_ge(w_in[n % STG][q], 16 * (n // STG + 1))
                r = slice(q * CH // 4, (q + 1) * CH // 4)
                nc.scalar.activation(whi[:, n // 2, n % 2, r], w_stage(n)[:, r], ACT.Copy,
                                     scale=W_SCALE).then_inc(hi_ok, 1)

            def store_normed(b):
                act.wait_ge(xn2_ok, HB * (b + 1))
                act.dma_start(xn_rows[b * S:b * S + S, :].rearrange("(h p) d -> p h d", p=P),
                              xn[:, HB * b:HB * b + HB, :]).then_inc(rows_out, 16)

            def store_residual(b):
                act.wait_ge(res_ok, b + 1)
                act.dma_start(out[b * S:b * S + S, :].rearrange("(h p) d -> p h d", p=P),
                              xs[:, HB * b:HB * b + HB, :]).then_inc(res_out, 16)

            def kv_copy(i):
                act.wait_ge(kv_mm, i + 1)
                nc.scalar.copy(kv[:, i * 4:i * 4 + 4, :].rearrange("p t c -> p (t c)"),
                               bank[4 + 2 * i][:, 0:4 * C]).then_inc(kv_ok, 1)

            ctxT_copy(0)
            act.wait_ge(wk_t, 1)
            nc.scalar.copy(wkT[0:C, :], bank[7][0:C, 0:C]).then_inc(wkT_ok, 1)
            pT_copy(0)
            kv_copy(0)
            kvT_copy(0)
            outT_copy(0)
            ctxT_copy(1)
            act.wait_ge(small_in, 16 * NSMALL)
            nc.scalar.activation(gates[:, :], gates[:, :], ACT.Tanh).then_inc(tanh_ok, 1)
            high_part(0, 0)
            high_part(0, 1)
            pT_copy(1)
            kvT_copy(1)
            for s in range(STEPS):
                if 0 <= s - 2 < B:
                    x2T_copy(s - 2)
                    store_normed(s - 2)
                if 0 <= s - 1 < B:
                    exponentials(s - 1)
                if s == 1:
                    kvT_copy(2)
                    kv_copy(1)
                    act.wait_ge(b1_t, 1)
                    nc.scalar.copy(b1_sb[:, :], bank[7][:, 0:E * FC]).then_inc(b1_ok, 1)
                    pT_copy(2)
                if 0 <= s - 2 < B:
                    second_exp(s - 2)
                if s < B:
                    normalise(s)
                if s + 1 < B:
                    outT_copy(s + 1)
                if s == 1:
                    for q in range(3):
                        high_part(1, q)
                    pT_copy(3)
                if s == STEPS - 1:
                    nc.scalar.preload_act_table(ACT.Gelu_apprx_tanh)
                if s >= B - 1:
                    combT_copy(s - (B - 1))
                for n, q in HIGH_AT[s]:
                    high_part(n, q)
                if s >= B:
                    store_residual(s - B)
            combT_copy(B - 1)
            store_residual(B - 2)

            act.wait_ge(b1_ok, 1)
            act.wait_ge(tiles_ok, 1)
            act.wait_ge(rows_out, 16 * B)
            tile = act.alloc_register("act_tile")
            act.reg_mov(tile, 0)
            counts = tile_counts(act)

            def token_high(n):
                act.wait_ge(xg_t, n)
                nc.scalar.activation(xhi[:, :, :].rearrange("p c t -> p (c t)"), bank[5][:, 0:D], ACT.Copy,
                                     scale=X_SCALE).then_inc(xhi_ok, 1)

            def expert_tile(e, quarters):
                g = act.snap(tile, min_val=0, max_val=MAXT - 1)
                for q in range(FC // 2):
                    act.wait_ge(h_mm, g * 4 + q + 1)
                    for r in range(2):
                        f = 2 * q + r
                        nc.scalar.activation(hact[:, f, :], bank[q][:, r * P:r * P + P], ACT.Gelu_apprx_tanh,
                                             bias=b1_sb[:, e * FC + f:e * FC + f + 1],
                                             scale=1.0 / (X_SCALE * W_SCALE)).then_inc(act_ok, 1)
                token_high(g + 2)
                for n, q in quarters:
                    high_part(n, q)
                act.wait_ge(y_mm, g + 1)
                act.wait_ge(ysb_free, g + 1)
                odd = act.snap(g & 1, min_val=0, max_val=1)
                nc.scalar.activation(ysb[:, bass.ds(odd, 1), :].rearrange("p a d -> p (a d)"), bank[4][:, 0:D],
                                     ACT.Copy, scale=wcur[:, bass.ds(odd, 1)]).then_inc(y_ok, 1)
                act.reg_add(tile, tile, 1)

            act.sem_inc(y_ok, 1)
            store_residual(B - 1)
            token_high(1)
            for e in range(E):
                tiles_e = tiles_of(act, counts, e)
                for j in range(PEEL):
                    quarters = splits(e, j)
                    with act.If(tiles_e > j):
                        expert_tile(e, quarters)
                    if quarters:
                        with act.Else():
                            for n, q in quarters:
                                high_part(n, q)
                with act.If(tiles_e > PEEL):
                    with act.Fori(PEEL, JT) as j:
                        with act.If(tiles_e > j):
                            expert_tile(e, ())

        @block.gpsimd
        def _(pool):
            pg = nc.gpsimd
            steps = [0]

            def link(ins):
                steps[0] += 1
                ins.then_inc(pool_step, 1)
                pool.wait_ge(pool_step, steps[0])

            pg.memset(ones[:, :], 1.0).then_inc(ones_ok, 1)
            link(pg.memset(ident[:, :], 0.0))
            pg.affine_select(out=ident[:, :], in_=ident[:, :], compare_op=ALU.not_equal, fill=1.0, base=0,
                             pattern=[[-1, P]], channel_multiplier=1).then_inc(ident_ok, 1)
            pg.memset(halfneg[:, :], -0.5)
            pg.memset(one[:, :], 1.0)
            link(pg.memset(negone[:, :], -1.0))

            def deviation(k, b):
                t = slice(HB * b, HB * b + HB)
                return pg.tensor_tensor(rstd[:, k, t], veps[:, k, t], halfneg[:, 0:HB], ALU.pow)

            def normed(k, b):
                link(deviation(k, b))
                for i in range(HB * b, HB * b + HB):
                    ins = pg.tensor_scalar(xn[:, i, :], xs[:, i, :], mneg[:, k, i:i + 1], rstd[:, k, i:i + 1],
                                           ALU.add, ALU.mult)
                    ins.then_inc(xn1_ok if k == 0 else xn2_ok, 1)

            for b in range(B):
                pool.wait_ge(mv1_ok, b + 1)
                normed(0, b)

            def constants():
                pool.wait_ge(ones_ok, 1)
                pg.affine_select(out=before[:, :], in_=ones[:, :], compare_op=ALU.is_gt, fill=0.0, base=0,
                                 pattern=[[1, P]], channel_multiplier=-1).then_inc(consts, 1)
                pg.memset(zeros[:, :], 0.0).then_inc(consts, 1)
                pg.iota(iota_e[:, :], [[1, E]], base=0, channel_multiplier=0,
                        allow_small_or_imprecise_dtypes=True).then_inc(consts, 1)
                pg.iota(giota[:, :], [[1, MAXT + 3]], base=0, channel_multiplier=0,
                        allow_small_or_imprecise_dtypes=True).then_inc(consts, 1)
                pg.iota(iota_r[:, :], [[1, P]], base=0, channel_multiplier=0,
                        allow_small_or_imprecise_dtypes=True).then_inc(consts, 1)
                pg.iota(iota_p[:, :], [[0, 1]], base=0, channel_multiplier=1,
                        allow_small_or_imprecise_dtypes=True).then_inc(consts, 1)
                pg.iota(vals[:, :, :, 0], [[P, TT], [0, KTOP]], base=-N, channel_multiplier=1,
                        allow_small_or_imprecise_dtypes=True).then_inc(consts, 1)

            def weights(b):
                t = slice(HB * b, HB * b + HB)
                pool.wait_ge(e2_ok, b + 1)
                link(pg.tensor_tensor(den[:, t], e2[:, t], one[:, :], ALU.add))
                link(pg.tensor_tensor(wk2[:, t, 0], den[:, t], negone[:, :], ALU.pow))
                link(pg.tensor_tensor(wk2[:, t, 1], e2[:, t], wk2[:, t, 0], ALU.mult))
                if b == 0:
                    pool.wait_ge(gslot_ok, 1)
                pg.tensor_tensor(vals[:, t, :, 1], wk2[:, t, :], gslot[:, 0:1].unsqueeze(1).broadcast_to([P, HB, KTOP]),
                                 ALU.mult).then_inc(vals_ok, 1)

            def place_rows(b):
                pool.wait_ge(slot_ok, b + 1)
                if b == 0:
                    pool.wait_ge(kvT_mm, 3)
                    pool.wait_ge(kv_mm, 2)
                else:
                    pool.wait_ge(place_mm, b)
                for h in range(HB):
                    for k in range(KTOP):
                        pg.tensor_scalar(atrow[:, h * KTOP + k, :], iota_r[:, :], rcf[:, HB * b + h, k, 0:1], None,
                                         ALU.is_equal).then_inc(atrow_ok, 1)

            def token_weights(b):
                t = slice(HB * b, HB * b + HB)
                pool.wait_ge(slot_ok, b + 1)
                link(pg.tensor_tensor(wmask[:, t, :, :].rearrange("p h k e -> p (h k) e"),
                                      mask[:, t, :, :].rearrange("p h k e -> p (h k) e"),
                                      wk2[:, t, :].rearrange("p h k -> p (h k)").unsqueeze(2).broadcast_to(
                                          [P, HB * KTOP, E]), ALU.mult))
                pg.tensor_tensor(comb[:, t, :], wmask[:, t, 0, :], wmask[:, t, 1, :], ALU.add).then_inc(comb_ok, 1)

            for s in range(STEPS):
                if s < B:
                    t = slice(HB * s, HB * s + HB)
                    pool.wait_ge(mv2_ok, s + 1)
                    link(deviation(1, s))
                    pg.tensor_tensor(nmr[:, t], mneg[:, 1, t], rstd[:, 1, t], ALU.mult).then_inc(rstd2_ok, 1)
                if s == 0:
                    constants()
                if 0 <= s - 2 < B:
                    weights(s - 2)
                if 0 <= s - 1 < B:
                    pool.wait_ge(mv3_ok, s)
                    pool.wait_ge(p_t, s)
                    normed(2, s - 1)
                if 0 <= s - 2 < B:
                    if s - 2 < B - 1:
                        place_rows(s - 2)
                    token_weights(s - 2)
            pool.wait_ge(pads_out, 32)
            pool.wait_ge(rows_out, 16 * B)
            pool.wait_ge(plan_ok, 1)
            total = pool.value_load(cendi[0:1, E - 1:E], min_val=KTOP * N // P, max_val=MAXT)

            def gather(g, first=False):
                col = pool.value_load(coli[0:1, bass.ds(g, 1)], min_val=0, max_val=E * JT - 1)
                if first:
                    pool.wait_ge(meta_ok, 1)
                else:
                    pool.wait_ge(xg_t, g)
                pg.tensor_copy(gidx[:, :], ids[:, bass.ds(col, 1)]).then_inc(gidx_ok, 1)
                pool.wait_ge(gidx_ok, 1)
                pool.indirect_dma_start(
                    out=xg[:, :], out_offset=None, in_=xn_rows,
                    in_offset=bass.IndirectOffsetOnAxis(gidx[:, :].bitcast(U32), 0)).then_inc(xg_in, 16)
                pool.sem_clear(gidx_ok)

            def rows_free(g, buf):
                col = pool.value_load(coli[0:1, bass.ds(g, 1)], min_val=0, max_val=E * JT - 1)
                pg.tensor_copy(wcur[:, buf:buf + 1], wts[:, bass.ds(col, 1)]).then_inc(ysb_free, 1)
                return col

            def add_rows(g, buf, col, first=False):
                pool.wait_ge(y_ok, g + 2)
                if not first:
                    pool.wait_ge(added, g * 16)
                pg.tensor_copy(sidx[:, :], ids[:, bass.ds(col, 1)]).then_inc(sidx_ok, 1)
                pool.wait_ge(sidx_ok, 1)
                pool.indirect_dma_start(
                    out=out, out_offset=bass.IndirectOffsetOnAxis(sidx[:, :].bitcast(U32), 0),
                    in_=ysb[:, buf, :], in_offset=None, compute_op=ALU.add).then_inc(added, 16)
                pool.sem_clear(sidx_ok)

            gather(0, first=True)
            gather(1)
            gather(2)
            pool.wait_ge(res_out, 16 * B)
            pool.wait_ge(meta_ok, 2)
            add_rows(0, 0, rows_free(0, 0), first=True)
            rows_free(1, 1)
            with pool.Fori(0, MAXT // 2) as pair:
                for r in range(2):
                    g = pool.snap(pair * 2 + (r + 1), min_val=1, max_val=MAXT)
                    with pool.If(g + 1 < total):
                        gather(g + 2)
                    with pool.If(g < total):
                        col = pool.value_load(coli[0:1, bass.ds(g, 1)], min_val=0, max_val=E * JT - 1)
                        add_rows(g, (r + 1) % 2, col)
                        rows_free(g + 1, r)
            pool.wait_ge(added, total * 16)

        @block.vector
        def _(dve):
            v = nc.vector
            steps = [0]

            def link(ins):
                steps[0] += 1
                ins.then_inc(dve_step, 1)
                dve.wait_ge(dve_step, steps[0])

            def mark(*instructions):
                for ins in instructions:
                    steps[0] += 1
                    ins.then_inc(dve_step, 1)
                return steps[0]

            def after(count):
                dve.wait_ge(dve_step, count)

            v.memset(ctxT[C:C + 1, :], 1.0).then_inc(ones_row, 1)
            mark(v.memset(zer8[:, :], 0.0))
            for e in range(E // 2):
                mark(v.memset(pow16[:, :].rearrange("p (h e) -> p h e", h=2)[:, :, e], 16.0 ** e))

            def tiles(b):
                return range(HB * b, HB * b + HB)

            def aggregate(k, b, eps, ready):
                t = slice(HB * b, HB * b + HB)
                dve.wait_ge(dve_step, steps[0])
                for i in tiles(b):
                    mark(v.bn_aggr(mv[:, k, i, :], st[:, k, i, :]))
                dve.wait_ge(dve_step, steps[0])
                mark(v.tensor_scalar(mneg[:, k, t], mv[:, k, t, 0], -1.0, None, ALU.mult))
                v.tensor_scalar(veps[:, k, t], mv[:, k, t, 1], eps, None, ALU.add).then_inc(ready, 1)

            def input_stats(b):
                dve.wait_ge(x_in[b], 16)
                for i in tiles(b):
                    mark(v.bn_stats(st[:, 0, i, :], xs[:, i, :]))
                aggregate(0, b, LN_EPS, mv1_ok)

            def sim_stats(b):
                for h in range(HB):
                    dve.wait_ge(sim_mm, HB * b + h + 1)
                    mark(v.bn_stats(st[:, 1, HB * b + h, :], bank[4 + h][:, 0:S]))
                aggregate(1, b, SIM_EPS, mv2_ok)

            def affine(b):
                dve.wait_ge(simn_ok, HB * (b + 1))
                link(v.tensor_tensor(sim[:, b % 2, :, :], sim[:, b % 2, :, :],
                                     neggamma[:, :].unsqueeze(1).broadcast_to([P, HB, S]), ALU.mult))
                for h in range(HB):
                    i = HB * b + h
                    v.tensor_tensor_reduce(sim[:, b % 2, h, :], sim[:, b % 2, h, :], negbeta[:, :], 1.0, 3.0e38,
                                           ALU.add, ALU.min, negmax[:, i:i + 1]).then_inc(aff_ok, 1)

            def residual_and_top_two(b, r):
                if b is not None:
                    t = slice(HB * b, HB * b + HB)
                    first = HB * b
                if r is not None:
                    u = slice(HB * r, HB * r + HB)
                    dve.wait_ge(lg_mm, r + 1)
                    routed = mark(v.tensor_tensor(
                        lg[:, u, :], bank[6][:, 0:HB * E].rearrange("p (h e) -> p h e", h=HB),
                        gb[:, :].unsqueeze(1).broadcast_to([P, HB, E]), ALU.add))
                if b is not None:
                    dve.wait_ge(exp_ok, HB * (b + 1))
                    done = mark(v.reciprocal(rsum[:, t], esum[:, t]))
                if r is not None:
                    after(routed)
                    routed = mark(*[v.max(mx[:, i, :], lg[:, i, :]) for i in tiles(r)])
                if b is not None:
                    after(done)
                    done = mark(v.tensor_scalar(coef[:, t], rsum[:, t], gates[:, 0:1], None, ALU.mult))
                if r is not None:
                    after(routed)
                    v.tensor_tensor(dif[:, u], mx[:, u, 1], mx[:, u, 0], ALU.subtract).then_inc(dif_ok, 1)
                    routed = mark(*[v.max_index(ix[:, i, :], mx[:, i, :], lg[:, i, :]) for i in tiles(r)])

                def add_attended(i):
                    return mark(v.scalar_tensor_tensor(
                        out=xs[:, i, :], in0=sim[:, b % 2, i - first, :], scalar=coef[:, i:i + 1], in1=xs[:, i, :],
                        op0=ALU.mult, op1=ALU.add))

                if b is not None:
                    after(done)
                    done = [add_attended(first)]
                if r is not None:
                    after(routed)
                    routed = mark(v.tensor_copy(ixf[:, u, :], ix[:, u, 0:KTOP]))
                if b is not None:
                    done.append(add_attended(first + 1))
                if r is not None:
                    after(routed)
                    routed = mark(v.tensor_tensor(
                        mask[:, u, :, :].rearrange("p h k e -> p (h k) e"),
                        iota_e[:, :].unsqueeze(1).broadcast_to([P, HB * KTOP, E]),
                        ixf[:, u, :].rearrange("p h k -> p (h k)").unsqueeze(2).broadcast_to([P, HB * KTOP, E]),
                        ALU.is_equal))
                if b is not None:
                    after(done[0])
                    seen = [mark(v.bn_stats(st[:, 2, first, :], xs[:, first, :]))]
                if r is not None:
                    after(routed)
                    v.tensor_tensor(mcount[:, u, :], mask[:, u, 0, :], mask[:, u, 1, :], ALU.add).then_inc(mask_ok, 1)
                if b is not None:
                    after(done[1])
                    mark(v.bn_stats(st[:, 2, first + 1, :], xs[:, first + 1, :]))
                    aggregate(2, b, LN_EPS, mv3_ok)

            def slots(b):
                t = slice(HB * b, HB * b + HB)
                last = b == B - 1
                dve.wait_ge(rank_mm, b + 1)
                if last:
                    plan = mark(v.tensor_scalar(cntr[:, :], bank[6][0:1, 64:64 + E], float(P - 1), None, ALU.add))
                done = mark(v.tensor_tensor(
                    rmask[:, t, :, :],
                    bank[6][:, 32:32 + HB * E].rearrange("p (h e) -> p h e", h=HB).unsqueeze(2).broadcast_to(
                        [P, HB, KTOP, E]),
                    mask[:, t, :, :], ALU.mult))
                if last:
                    after(plan)
                    plan = mark(v.tensor_scalar(ntile[:, :], cntr[:, :], 7, None, ALU.logical_shift_right))
                after(done)
                with nc.allow_low_precision(reason="whole numbers below 1024"):
                    done = mark(v.tensor_reduce(ranki[:, t, :], rmask[:, t, :, :], mybir.AxisListType.X, ALU.add))
                if last:
                    after(plan)
                    plan = mark(v.tensor_copy(ntf[:, :], ntile[:, :]))
                after(done)
                done = mark(v.tensor_scalar(rhigh[:, t, :], ranki[:, t, :], 7, None, ALU.logical_shift_right))
                mark(v.tensor_scalar(rc[:, t, :, 0], ranki[:, t, :], P - 1, None, ALU.bitwise_and))
                if last:
                    after(plan)
                    plan = mark(v.tensor_tensor_scan(cend[:, :], ntf[:, :], zer8[:, :], 0.0, ALU.add, ALU.add))
                    counted = mark(v.tensor_tensor(npow[:, :], ntf[:, :], pow16[:, :], ALU.mult))
                    mark(v.tensor_scalar(ngap[:, :], ntf[:, :], -1.0, float(JT), ALU.mult, ALU.add))
                after(done)
                done = mark(v.scalar_tensor_tensor(out=rc[:, t, :, 1], in0=ix[:, t, 0:KTOP].bitcast(I32), scalar=3,
                                                   in1=rhigh[:, t, :], op0=ALU.logical_shift_left,
                                                   op1=ALU.bitwise_or))
                if last:
                    after(plan)
                    plan = mark(v.tensor_tensor(past[:, :, :],
                                                cend[:, :].unsqueeze(1).broadcast_to([1, MAXT + 3, E]),
                                                giota[:, :].unsqueeze(2).broadcast_to([1, MAXT + 3, E]), ALU.is_le))
                after(done)
                v.tensor_copy(rcf[:, t, :, :], rc[:, t, :, :]).then_inc(slot_ok, 1)
                if last:
                    after(counted)
                    with nc.allow_low_precision(reason="whole numbers below 65536"):
                        v.tensor_reduce(packed[:, :], npow[:, :].rearrange("p (h e) -> p h e", h=2),
                                        mybir.AxisListType.X, ALU.add).then_inc(tiles_ok, 1)
                dve.wait_ge(slot_ok, b + 1)
                if b == 0:
                    dve.wait_ge(kvT_mm, 3)
                    dve.wait_ge(kv_mm, 2)
                else:
                    dve.wait_ge(place_mm, b)
                full = [P, HB * KTOP, 2, E * JT]
                hot = mark(v.tensor_tensor(
                    colhot[:, :, :], iota_r[:, 0:E * JT].unsqueeze(1).broadcast_to([P, HB * KTOP, E * JT]),
                    rcf[:, t, :, 1].rearrange("p h k -> p (h k)").unsqueeze(2).broadcast_to(
                        [P, HB * KTOP, E * JT]), ALU.is_equal))
                if last:
                    v.tensor_tensor(atrow[:, :, :], iota_r[:, :].unsqueeze(1).broadcast_to([P, HB * KTOP, P]),
                                    rcf[:, t, :, 0].rearrange("p h k -> p (h k)").unsqueeze(2).broadcast_to(
                                        [P, HB * KTOP, P]), ALU.is_equal).then_inc(atrow_ok, HB * KTOP)
                after(hot)
                dve.wait_ge(vals_ok, b + 1)
                v.tensor_tensor(atcol[:, :, :, :], colhot[:, :, :].unsqueeze(2).broadcast_to(full),
                                vals[:, t, :, :].rearrange("p h k v -> p (h k) v").unsqueeze(3).broadcast_to(full),
                                ALU.mult).then_inc(atcol_ok, 1)
                if last:
                    link(v.tensor_tensor(pastn[:, :, :], past[:, :, :],
                                         ngap[:, :].unsqueeze(1).broadcast_to([1, MAXT + 3, E]), ALU.mult))
                    mark(v.tensor_copy(cendi[:, :], cend[:, :]))
                    link(v.tensor_reduce(sg[:, :], pastn[:, :, :], mybir.AxisListType.X, ALU.add))
                    link(v.tensor_tensor(col1[:, :], giota[:, :], sg[:, :], ALU.add))
                    v.tensor_scalar(coli[:, :], col1[:, :], float(E * JT - 1), None, ALU.min).then_inc(plan_ok, 1)

            def bias_out(b):
                t = slice(HB * b, HB * b + HB)
                dve.wait_ge(b2_mm, b + 1)
                v.scalar_tensor_tensor(out=xs[:, t, :].rearrange("p h d -> p (h d)"), in0=bank[b % 2 * 2][:, :],
                                       scalar=gates[:, 1:2], in1=xs[:, t, :].rearrange("p h d -> p (h d)"),
                                       op0=ALU.mult, op1=ALU.add).then_inc(res_ok, 1)

            def low_part(n, q):
                dve.wait_ge(w_in[n % STG][q], 16 * (n // STG + 1))
                r = slice(q * CH // 4, (q + 1) * CH // 4)
                dve.wait_ge(hi_ok, 4 * n + q + 1)
                v.scalar_tensor_tensor(out=wlo[:, n // 2, n % 2, r], in0=w_stage(n)[:, r], scalar=W_SCALE,
                                       in1=whi[:, n // 2, n % 2, r], op0=ALU.mult,
                                       op1=ALU.subtract).then_inc(lo_ok, 1)

            for b in range(B):
                input_stats(b)
            dve.wait_ge(small_in, 16 * NSMALL)
            mark(v.tensor_scalar(neggamma[:, :], neggamma[:, :], -1.0, None, ALU.mult))
            mark(v.tensor_scalar(negbeta[:, :], negbeta[:, :], -1.0, None, ALU.mult))

            for s in range(STEPS):
                if 0 <= s - 1 < B:
                    affine(s - 1)
                if s < B:
                    sim_stats(s)
                if s == 0:
                    dve.wait_ge(tanh_ok, 1)
                    v.tensor_scalar(gslot[:, :], gates[:, 1:2], 1.0 / (H_SCALE * W_SCALE), None,
                                    ALU.mult).then_inc(gslot_ok, 1)
                if s == B:
                    bias_out(0)
                if s == B + 1:
                    bias_out(1)
                for n, q in LOW_AT[s]:
                    low_part(n, q)
                if s >= 1:
                    residual_and_top_two(s - 1 if s - 1 < B else None, s - 2 if s >= 2 else None)
                if 0 <= s - 2 < B:
                    slots(s - 2)

            dve.wait_ge(place_mm, B)
            link(v.tensor_scalar(padid[:, :], bank[7][:, 0:E * JT], 0.0, iota_p[:, 0:1], ALU.is_equal, ALU.mult))
            v.scalar_tensor_tensor(out=ids[:, :], in0=bank[7][:, 0:E * JT], scalar=float(N), in1=padid[:, :],
                                   op0=ALU.add, op1=ALU.add).then_inc(meta_ok, 1)
            v.tensor_copy(wts[:, :], bank[7][:, E * JT:2 * E * JT]).then_inc(meta_ok, 1)

            def token_low(n):
                dve.wait_ge(xhi_ok, n)
                v.scalar_tensor_tensor(out=xlo[:, :, :].rearrange("p c t -> p (c t)"), in0=bank[5][:, 0:D],
                                       scalar=X_SCALE, in1=xhi[:, :, :].rearrange("p c t -> p (c t)"),
                                       op0=ALU.mult, op1=ALU.subtract).then_inc(xlo_ok, 1)

            def expert_tile(quarters):
                g = dve.snap(tile, min_val=0, max_val=MAXT - 1)
                for q in range(FC // 2):
                    f = slice(2 * q, 2 * q + 2)
                    dve.wait_ge(act_ok, g * FC + 2 * q + 2)
                    v.tensor_scalar(hhi[:, f, :], hact[:, f, :], H_SCALE, None, ALU.mult).then_inc(hhi_ok, 1)
                    dve.wait_ge(hhi_ok, g * 4 + q + 1)
                    v.scalar_tensor_tensor(out=hlo[:, f, :], in0=hact[:, f, :], scalar=H_SCALE,
                                           in1=hhi[:, f, :], op0=ALU.mult, op1=ALU.subtract).then_inc(hsplit_ok, 1)
                token_low(g + 2)
                for n, q in quarters:
                    low_part(n, q)
                dve.reg_add(tile, tile, 1)

            bias_out(B - 2)
            bias_out(B - 1)
            low_part(1, 3)
            for q in range(3):
                low_part(2, q)
            tile = dve.alloc_register("dve_tile")
            dve.reg_mov(tile, 0)
            dve.wait_ge(tiles_ok, 1)
            counts = tile_counts(dve)
            token_low(1)
            low_part(2, 3)
            for e in range(E):
                tiles_e = tiles_of(dve, counts, e)
                for j in range(PEEL):
                    quarters = splits(e, j)
                    with dve.If(tiles_e > j):
                        expert_tile(quarters)
                    if quarters:
                        with dve.Else():
                            for n, q in quarters:
                                low_part(n, q)
                with dve.If(tiles_e > PEEL):
                    with dve.Fori(PEEL, JT) as j:
                        with dve.If(tiles_e > j):
                            expert_tile(())

        @block.tensor
        def _(pe):
            pe.wait_ge(ident_ok, 1)

            def keep_warm(n, o=1):
                for _ in range(n):
                    pe.matmul(bank[o][:, 0:P], ones[:, :], ones[:, :], start=True, stop=True)

            def context(i):
                for t in range(4):
                    m = pe.transpose(bank[1 + 5 * i][0:C, t * P:t * P + P], ctx_sb[:, 4 * i + t, :], ident[:, :])
                m.then_inc(ctx_t, 1)

            def keys(i):
                at, n, o = KEYS[i]
                pe.wait_ge(ctxT_ok, 1 + i // 2)
                pe.matmul(bank[o][0:C, 0:n], wkT[:, :], ctxT[:, at:at + n],
                          start=True, stop=True).then_inc(kvT_mm, 1)

            def values(i):
                pe.wait_ge(ctxT_ok, i + 1)
                for t in range(4):
                    m = pe.matmul(bank[4 + 2 * i][:, t * C:t * C + C], ctxT[:, (4 * i + t) * P:(4 * i + t + 1) * P],
                                  wkT[:, :], start=True, stop=True)
                m.then_inc(kv_mm, 1)

            def transpose_p(b):
                pe.wait_ge(xn1_ok, HB * (b + 1))
                if b >= 1:
                    pe.wait_ge(pT_ok, b)
                for h in range(HB):
                    for c in range(DC):
                        t = pe.transpose(bank[0][:, c * S + h * P:c * S + h * P + P],
                                         xn[:, HB * b + h, c * P:c * P + P], ident[:, :])
                t.then_inc(p_t, 1)

            def attend(b):
                pe.wait_ge(pT_ok, b + 1)
                pe.wait_ge(kv_ok, 1 + b // 2)
                if b >= 1:
                    pe.wait_ge(outT_ok, b)
                for c in range(DC):
                    m = pe.matmul(bank[2][0:C, 0:S], kv[:, HB * b + c, :], pT[:, c, :],
                                  start=(c == 0), stop=(c == DC - 1))
                m.then_inc(out_mm, 1)

            def similarities(b):
                pe.wait_ge(outT_ok, b + 1)
                pe.wait_ge(kvT_ok, min(b, 2) + 1)
                if b >= 1:
                    pe.wait_ge(simn_ok, HB * b)
                for h in range(HB):
                    pe.matmul(bank[4 + h][:, 0:S], outT[:, h * P:h * P + P], kvT[:, b * S:b * S + S],
                              start=True, stop=True).then_inc(sim_mm, 1)

            def logits(b):
                if b == 0:
                    pe.wait_ge(kvT_ok, 3)
                    pe.wait_ge(gate_in, 48)
                else:
                    pe.wait_ge(x2T_ok, HB * b)
                for h in range(HB):
                    pe.wait_ge(xn2_ok, HB * b + h + 1)
                    for c in range(DC):
                        t = pe.transpose(bank[3 - 2 * h][:, c * P:c * P + P], xn[:, HB * b + h, c * P:c * P + P],
                                         ident[:, :])
                    t.then_inc(x2_t, 1)
                if b == 0:
                    keep_warm(6, 7)
                    pe.wait_ge(kv_ok, 2)
                else:
                    pe.wait_ge(slot_ok, b)
                for h in range(HB):
                    pe.wait_ge(x2T_ok, HB * b + h + 1)
                    for c in range(DC):
                        m = pe.matmul(bank[6][:, h * E:h * E + E], x2T[:, h, c, :], gw[:, c, :],
                                      start=(c == 0), stop=(c == DC - 1))
                m.then_inc(lg_mm, 1)

            def ranks(b):
                pe.wait_ge(mask_ok, b + 1)
                if b == 0:
                    pe.wait_ge(consts, NCONST)
                for h in range(HB):
                    i = HB * b + h
                    o = bank[6][:, 32 + h * E:32 + h * E + E]
                    m = pe.matmul(o, before[:, :], mcount[:, i, :], start=True, stop=(i == 0))
                    for k in range(i):
                        m = pe.matmul(o, ones[:, :], mcount[:, k, :], start=False, stop=(k == i - 1))
                if b == B - 1:
                    for k in range(TT):
                        m = pe.matmul(bank[6][:, 64:64 + E], ones[:, :], mcount[:, k, :],
                                      start=(k == 0), stop=(k == TT - 1))
                m.then_inc(rank_mm, 1)

            def place(b):
                pe.wait_ge(atrow_ok, HB * KTOP * (b + 1))
                pe.wait_ge(atcol_ok, b + 1)
                if b == 0:
                    pe.wait_ge(b1_ok, 1)
                for t in range(HB * KTOP):
                    m = pe.matmul(bank[7][:, 0:2 * E * JT], atrow[:, t, :], atcol[:, t, :, :],
                                  start=(b == 0 and t == 0), stop=(b == B - 1 and t == HB * KTOP - 1))
                m.then_inc(place_mm, 1)

            def bias_rows(b):
                pe.wait_ge(comb_ok, b + 1)
                o = bank[b % 2 * 2]
                if b < 2:
                    pe.wait_ge(outT_ok if b else pT_ok, B)
                else:
                    pe.wait_ge(res_ok, b - 1)
                for h in range(HB):
                    t = pe.transpose(o[0:E, h * P:h * P + P], comb[:, HB * b + h, :], ident[:, :])
                t.then_inc(comb_t, 1)
                keep_warm(6)
                pe.wait_ge(combT_ok, b + 1)
                for h in range(HB):
                    m = pe.matmul(o[:, h * D:h * D + D], combT[:, h * P:h * P + P], b2_sb[:, :],
                                  start=True, stop=True)
                m.then_inc(b2_mm, 1)

            pe.wait_ge(ones_ok, 1)
            keep_warm(36, 7)
            pe.wait_ge(ctx_in, 16)
            context(0)
            pe.wait_ge(wk_in, 32)
            pe.transpose(bank[7][0:C, 0:C], wk_sb[:, :], ident[0:C, 0:C]).then_inc(wk_t, 1)
            transpose_p(0)
            pe.wait_ge(wkT_ok, 1)
            pe.wait_ge(ones_row, 1)
            values(0)
            keys(0)
            attend(0)
            context(1)
            similarities(0)
            transpose_p(1)
            keys(1)
            pe.wait_ge(wkT_ok, 1)
            keep_warm(16, 7)
            for s in range(STEPS):
                if 0 <= s - 2 < B:
                    logits(s - 2)
                if 0 <= s - 3 < B:
                    place(s - 3)
                if 0 <= s - 2 < B:
                    keep_warm((0, 0, 36, 16, 16, 6)[s])
                    ranks(s - 2)
                if s + 1 < B:
                    attend(s + 1)
                    if s >= 1:
                        keep_warm(6)
                    similarities(s + 1)
                if s == 0:
                    keys(2)
                    values(1)
                    pe.wait_ge(small_in, 16 * NSMALL)
                    pe.transpose(bank[7][:, 0:E * FC], b1_rows[:, :], ident[0:E * FC, 0:E * FC]).then_inc(b1_t, 1)
                if s + 2 < B:
                    transpose_p(s + 2)
                if s >= B - 1:
                    bias_rows(s - (B - 1))
                if s >= 1:
                    keep_warm(12)
            place(B - 1)
            bias_rows(B - 1)
            keep_warm(52)
            pe.wait_ge(tiles_ok, 1)
            tile = pe.alloc_register("pe_tile")
            pe.reg_mov(tile, 0)
            counts = tile_counts(pe)

            def transpose_tokens(n):
                pe.wait_ge(xg_in, n * 16)
                for c in range(DC):
                    t = pe.transpose(bank[5][:, c * P:c * P + P], xg[:, c * P:c * P + P], ident[:, :])
                t.then_inc(xg_t, 1)

            def expert_tile(e):
                g = pe.snap(tile, min_val=0, max_val=MAXT - 1)
                pe.wait_ge(xlo_ok, g + 1)
                for q in range(FC // 2):
                    for r in range(2):
                        f = 2 * q + r
                        k = 0
                        for c in range(DC):
                            w = slice(c * F + f * P, c * F + f * P + P)
                            for wt, xt in ((whi, xhi), (whi, xlo), (wlo, xhi)):
                                m = pe.matmul(bank[q][:, r * P:r * P + P], wt[:, e, 0, w], xt[:, c, :],
                                              start=(k == 0), stop=(k == 3 * DC - 1))
                                k += 1
                    m.then_inc(h_mm, 1)
                pe.wait_ge(hi_ok, 8 * e + 8)
                pe.wait_ge(lo_ok, 8 * e + 8)
                pe.wait_ge(y_ok, g + 1)
                transpose_tokens(g + 2)
                for f in range(FC):
                    if f % 2 == 0:
                        pe.wait_ge(hsplit_ok, g * 4 + f // 2 + 1)
                    for ht, wt in ((hhi, whi), (hhi, wlo), (hlo, whi)):
                        m = pe.matmul(bank[4][:, 0:D], ht[:, f, :], wt[:, e, 1, f * D:f * D + D],
                                      start=(f == 0 and ht is hhi and wt is whi),
                                      stop=(f == FC - 1 and ht is hlo))
                m.then_inc(y_mm, 1)
                pe.reg_add(tile, tile, 1)

            transpose_tokens(1)
            keep_warm(14)
            pe.wait_ge(res_ok, B)
            for e in range(E):
                tiles_e = tiles_of(pe, counts, e)
                pe.wait_ge(hi_ok, 8 * e + 4)
                pe.wait_ge(lo_ok, 8 * e + 4)
                for j in range(PEEL):
                    with pe.If(tiles_e > j):
                        expert_tile(e)
                with pe.If(tiles_e > PEEL):
                    with pe.Fori(PEEL, JT) as j:
                        with pe.If(tiles_e > j):
                            expert_tile(e)


_INS = ['x', 'ctx_512', 'g_xattn', 'g_ffn', 'L0_xattn_W_k', 'L0_xattn_b_k', 'L0_xattn_ln_gamma', 'L0_xattn_ln_beta',
        'L0_ffn_gate_w', 'L0_ffn_gate_b', 'L0_ffn_w1', 'L0_ffn_b1', 'L0_ffn_w2', 'L0_ffn_b2']


def kernel(**inputs):
    import numpy as _np
    import concourse.bacc as _bacc
    from concourse import mybir as _mybir
    from concourse.bass_utils import run_bass_kernel_spmd as _run

    nc = _bacc.Bacc("TRN2", target_bir_lowering=False, num_devices=1)
    arrays, args = {}, []
    for name in _INS:
        a = _np.ascontiguousarray(inputs[name])
        arrays[f"in_{name}"] = a
        args.append(nc.dram_tensor(f"in_{name}", a.shape, _mybir.dt.from_np(a.dtype), kind="ExternalInput").ap())
    B, S, D = inputs['x'].shape
    out = nc.dram_tensor("out_rows", (B * S + 128, D), _mybir.dt.float32, kind="ExternalOutput").ap()
    gated_block(nc, *args, out)
    r = _run(nc, [arrays], core_ids=[0])
    return r.results[0]["out_rows"][:B * S].reshape(B, S, D)
```
